# Optimizing a Trainium2 kernel written in Bass

```python
import numpy as np
import jax
import jax.numpy as jnp

def _softmax(x, axis=-1):
    return jax.nn.softmax(x, axis=axis)

def _gelu(x):
    return jax.nn.gelu(x, approximate=True)

def _silu(x):
    return jax.nn.silu(x)

def _sigmoid(x):
    return jax.nn.sigmoid(x)

def _layernorm(x, axis=-1, eps=1e-05):
    m = jnp.mean(x, axis=axis, keepdims=True)
    v = jnp.var(x, axis=axis, keepdims=True)
    return (x - m) / jnp.sqrt(v + eps)

def _scatter_add(tgt, idx, src, axis=0):
    return tgt.at[idx].add(src)

def _segment_sum(src, seg, n):
    return jax.ops.segment_sum(src, seg, n)
kernel_name = 'mk_macaron_d1_jaxref_r8_b718cc'

def setup_inputs(seed: int=0):
    np.random.seed(seed)
    _w = jnp.asarray

    def _L0_attn_setup():
        import jax, jax.numpy as jnp
        import numpy as np
        import math
        D_MODEL = 128
        N_HEADS = 16
        D_HEAD = D_MODEL // N_HEADS
        MAX_SEQ_LEN = 256
        BASE = 10000.0

        def _rope_tables(L):
            pos = jnp.arange(L, dtype=jnp.float32)[:, None]
            freqs = jnp.exp(-math.log(BASE) * jnp.arange(0, D_HEAD, 2, dtype=jnp.float32) / D_HEAD)
            angles = pos * freqs
            return (jnp.sin(angles), jnp.cos(angles))

        def _apply_rope(x, sin, cos):
            s = sin[None, :, None, :]
            c = cos[None, :, None, :]
            x_even, x_odd = (x[..., ::2], x[..., 1::2])
            rot_even = x_even * c - x_odd * s
            rot_odd = x_even * s + x_odd * c
            return jnp.stack([rot_even, rot_odd], axis=-1).reshape(x.shape)
        key = jax.random.key(seed)
        k0, k1, k2, k3, k4 = jax.random.split(key, 5)
        B, L = (2, 256)
        scale = 1.0 / math.sqrt(D_MODEL)
        return {'x': jax.random.normal(k0, (B, L, D_MODEL), dtype=jnp.float32), 'W_q': jax.random.normal(k1, (D_MODEL, D_MODEL), dtype=jnp.float32) * scale, 'W_k': jax.random.normal(k2, (D_MODEL, D_MODEL), dtype=jnp.float32) * scale, 'W_v': jax.random.normal(k3, (D_MODEL, D_MODEL), dtype=jnp.float32) * scale, 'W_o': jax.random.normal(k4, (D_MODEL, D_MODEL), dtype=jnp.float32) * scale}
    _L0_attn_in = _L0_attn_setup()

    def _L0_ffn_setup():
        import jax, jax.numpy as jnp
        import numpy as np
        B, S, H, F, E = (1, 256, 128, 256, 8)

        def _swiglu(x, wg, wu, wd):
            return jax.nn.silu(x @ wg.T) * (x @ wu.T) @ wd.T
        key = jax.random.key(seed)
        ks = jax.random.split(key, 8)
        sc = 1.0 / np.sqrt(H)
        scf = 1.0 / np.sqrt(F)
        return {'hidden_states': jax.random.normal(ks[0], (B, S, H), jnp.float32), 'gate_w': jax.random.normal(ks[1], (E, H), jnp.float32) * sc, 'shared_gate': jax.random.normal(ks[2], (F, H), jnp.float32) * sc, 'shared_up': jax.random.normal(ks[3], (F, H), jnp.float32) * sc, 'shared_down': jax.random.normal(ks[4], (H, F), jnp.float32) * scf, 'r_gate': jax.random.normal(ks[5], (E, F, H), jnp.float32) * sc, 'r_up': jax.random.normal(ks[6], (E, F, H), jnp.float32) * sc, 'r_down': jax.random.normal(ks[7], (E, H, F), jnp.float32) * scf}
    _L0_ffn_in = _L0_ffn_setup()
    _d = {'L0_attn_x': _L0_attn_in['x'], 'L0_attn_W_q': _L0_attn_in['W_q'], 'L0_attn_W_k': _L0_attn_in['W_k'], 'L0_attn_W_v': _L0_attn_in['W_v'], 'L0_attn_W_o': _L0_attn_in['W_o'], 'L0_ffn_gate_w': _L0_ffn_in['gate_w'], 'L0_ffn_shared_gate': _L0_ffn_in['shared_gate'], 'L0_ffn_shared_up': _L0_ffn_in['shared_up'], 'L0_ffn_shared_down': _L0_ffn_in['shared_down'], 'L0_ffn_r_gate': _L0_ffn_in['r_gate'], 'L0_ffn_r_up': _L0_ffn_in['r_up'], 'L0_ffn_r_down': _L0_ffn_in['r_down']}
    _x0 = _d['L0_attn_x']
    _d['L0_attn_x'] = jax.random.normal(jax.random.fold_in(jax.random.key(seed), 1), (8, 256, 128), dtype=_x0.dtype)
    del _x0
    return _d

def reference(L0_attn_x, L0_attn_W_q, L0_attn_W_k, L0_attn_W_v, L0_attn_W_o, L0_ffn_gate_w, L0_ffn_shared_gate, L0_ffn_shared_up, L0_ffn_shared_down, L0_ffn_r_gate, L0_ffn_r_up, L0_ffn_r_down):

    def _L0_attn_ref(x, W_q, W_k, W_v, W_o):
        import jax, jax.numpy as jnp
        import numpy as np
        import math
        D_MODEL = 128
        N_HEADS = 16
        D_HEAD = D_MODEL // N_HEADS
        MAX_SEQ_LEN = 256
        BASE = 10000.0

        def _rope_tables(L):
            pos = jnp.arange(L, dtype=jnp.float32)[:, None]
            freqs = jnp.exp(-math.log(BASE) * jnp.arange(0, D_HEAD, 2, dtype=jnp.float32) / D_HEAD)
            angles = pos * freqs
            return (jnp.sin(angles), jnp.cos(angles))

        def _apply_rope(x, sin, cos):
            s = sin[None, :, None, :]
            c = cos[None, :, None, :]
            x_even, x_odd = (x[..., ::2], x[..., 1::2])
            rot_even = x_even * c - x_odd * s
            rot_odd = x_even * s + x_odd * c
            return jnp.stack([rot_even, rot_odd], axis=-1).reshape(x.shape)
        B, L, _ = x.shape
        sin, cos = _rope_tables(L)
        q = (x @ W_q.T).reshape(B, L, N_HEADS, D_HEAD)
        k = (x @ W_k.T).reshape(B, L, N_HEADS, D_HEAD)
        v = (x @ W_v.T).reshape(B, L, N_HEADS, D_HEAD)
        q = _apply_rope(q, sin, cos)
        k = _apply_rope(k, sin, cos)
        scores = jnp.einsum('blhd,bshd->bhls', q, k) / math.sqrt(D_HEAD)
        weights = jax.nn.softmax(scores, axis=-1)
        out = jnp.einsum('bhls,bshd->blhd', weights, v).reshape(B, L, D_MODEL)
        return out @ W_o.T

    def _L0_ffn_ref(hidden_states, gate_w, shared_gate, shared_up, shared_down, r_gate, r_up, r_down):
        import jax, jax.numpy as jnp
        import numpy as np
        B, S, H, F, E = (1, 256, 128, 256, 8)

        def _swiglu(x, wg, wu, wd):
            return jax.nn.silu(x @ wg.T) * (x @ wu.T) @ wd.T
        b, s, h = hidden_states.shape
        x = hidden_states.reshape(-1, h)
        shared_out = _swiglu(x, shared_gate, shared_up, shared_down)
        logits = x @ gate_w.T
        top_id = jnp.argmax(logits, axis=-1)
        score = jax.nn.sigmoid(jnp.max(logits, axis=-1))
        xs = x * score[:, None]

        def body(acc, ws):
            wg, wu, wd, e = ws
            xe = jnp.where((top_id == e)[:, None], xs, 0.0)
            return (acc + _swiglu(xe, wg, wu, wd), None)
        acc0 = jnp.zeros_like(x)
        routed_out, _ = jax.lax.scan(body, acc0, (r_gate, r_up, r_down, jnp.arange(E)))
        return (shared_out + routed_out).reshape(b, s, h)
    x = L0_attn_x
    x = x + 0.5 * _L0_ffn_ref(_layernorm(x, axis=-1), L0_ffn_gate_w, L0_ffn_shared_gate, L0_ffn_shared_up, L0_ffn_shared_down, L0_ffn_r_gate, L0_ffn_r_up, L0_ffn_r_down)
    x = x + _L0_attn_ref(_layernorm(x, axis=-1), L0_attn_W_q, L0_attn_W_k, L0_attn_W_v, L0_attn_W_o)
    x = x + 0.5 * _L0_ffn_ref(_layernorm(x, axis=-1), L0_ffn_gate_w, L0_ffn_shared_gate, L0_ffn_shared_up, L0_ffn_shared_down, L0_ffn_r_gate, L0_ffn_r_up, L0_ffn_r_down)
    return x

_drawn_inputs = setup_inputs


def setup_inputs(seed=0):
    import zlib

    import numpy as np

    out = dict(_drawn_inputs(seed))
    spreads = {}
    factors = {}
    for name, (base, spread) in spreads.items():
        noise = np.random.default_rng([zlib.crc32(name.encode()), seed]).standard_normal(out[name].shape)
        drawn = base * np.exp(spread * noise) if base else spread * noise
        out[name] = jnp.asarray(drawn.astype(out[name].dtype))
    for name, factor in factors.items():
        out[name] = (out[name] * factor).astype(out[name].dtype)
    return out
```

```python
from contextlib import ExitStack

import concourse.bass as bass
from concourse import mybir
from concourse.alu_op_type import AluOpType as ALU
import numpy as np

ACT = mybir.ActivationFunctionType
AX = mybir.AxisListType
F32 = mybir.dt.float32
BF16 = mybir.dt.bfloat16
I32 = mybir.dt.int32
U32 = mybir.dt.uint32

P = 128
D = 128
B, L = 8, 256
H, DH = 16, 8
F = 256
E = 8
N = B * L
TILES = N // P
CHUNK = 4
CHUNKS = TILES // CHUNK
SLOT_TILES = TILES + E - 1
LOAD = 4
LOADS = -(-SLOT_TILES // LOAD)
EPS = 1e-5
KROWS = 64
MCOL = 6 * DH
QUADS = H // 4


def build(nc, x_in, wqkv_in, wo_in, wgate_in, shgu_in, shdn_in, rgu_in, rdn_in, tab_in, tabb_in, out):
    ctx = ExitStack()
    with ctx:
        def sb(name, shape, dt):
            return ctx.enter_context(nc.sbuf_tensor(name, shape, dt))

        def sem(name):
            return ctx.enter_context(nc.semaphore(name))

        def sems(name, n):
            return [sem(f"{name}{i}") for i in range(n)]

        x = sb("x", [P, TILES, D], F32)
        wqkv = sb("wqkv", [D, 3 * D], F32)
        wo = sb("wo", [D, D], F32)
        wgate = sb("wgate", [D, 32], F32)
        shgu = sb("shgu", [D, 2 * F], F32)
        shdn = sb("shdn", [P, 2, D], F32)
        rgu = sb("rgu", [D, E * 2 * F], F32)
        rdn = sb("rdn", [P, E * 2 * D], F32)
        tab = sb("tab", [P, TAB_COLS], F32)
        tabb = sb("tabb", [P, TABB_COLS], BF16)
        ident = tab[:, 0:P]
        cos = tab[:, P:P + 512].rearrange("p (t n) -> p t n", t=2)
        sin = tab[:, P + 512:P + 1024].rearrange("p (t n) -> p t n", t=2)
        o = P + 1024
        steps128 = tab[:, o:o + 16]
        before = tab[:, o + 16:o + 80].rearrange("p (e f) -> p e f", e=E)
        eminus8 = tab[:, o + 80:o + 88]
        tile_no = tab[:, o + 88:o + 88 + SLOT_TILES]
        identb = tabb[:, 0:P]
        upper = tabb[:, P:2 * P]
        onesb = tabb[:, 2 * P:3 * P]

        stats = sb("stats", [P, TILES, 6], F32)
        meanvar = sb("meanvar", [P, TILES, 2], F32)
        rstd = sb("rstd", [P, TILES], F32)
        neghalf = sb("neghalf", [P, TILES], F32)
        xn = sb("xn", [P, TILES, D], F32)
        xnT = sb("xnT", [D, N], F32)
        lgT = sb("lgT", [P, 512], F32)
        lg = sb("lg", [P, TILES, E], F32)
        top = sb("top", [P, TILES], F32)
        is_top = sb("is_top", [P, TILES, E], F32)
        first_top = sb("first_top", [P, TILES], F32)
        onehot = sb("onehot", [P, TILES, E], F32)
        onehotb = sb("onehotb", [P, TILES, E], BF16)
        tanh_half = sb("tanh_half", [P, TILES], F32)
        score = sb("score", [P, TILES], F32)
        total = sb("total", [P, E], F32)
        over = sb("over", [P, E, 16], F32)
        etiles = sb("etiles", [P, E], F32)
        etb = sb("etb", [P, E, E], F32)
        estart = sb("estart", [P, E], F32)
        estart128 = sb("estart128", [P, E], F32)
        eend = sb("eend", [P, E], F32)
        slot8 = sb("slot8", [P, TILES, E], F32)
        slotf = sb("slotf", [P, TILES], F32)
        slot = sb("slot", [P, TILES], U32)
        ended = sb("ended", [1, SLOT_TILES, E], F32)
        expertf = sb("expertf", [1, SLOT_TILES], F32)
        expert = sb("expert", [1, SLOT_TILES], I32)
        xs = sb("xs", [P, TILES, D], F32)
        sgate = sb("sgate", [P, 2, 512], F32)
        sh = sb("sh", [P, 2, 2, 512], F32)
        xg = sb("xg", [P, LOADS * LOAD, D], F32)
        xgs = sb("xgs", [P, 2, D], F32)
        xgT = sb("xgT", [P, 2, P], F32)
        rsg = sb("rsg", [P, 2, F], F32)
        rh = sb("rh", [P, 2, F], F32)
        rhT = sb("rhT", [P, 2, 2, P], F32)
        ys = sb("ys", [P, SLOT_TILES, D], F32)
        yg = xs
        xs_dram = nc.dram_tensor("xs_sorted", (SLOT_TILES * P, D), F32, kind="Internal").ap()
        ys_dram = nc.dram_tensor("ys_sorted", (SLOT_TILES * P, D), F32, kind="Internal").ap()

        stats2 = sb("stats2", [P, 2, 6], F32)
        meanvar2 = sb("meanvar2", [P, 2, 2, 2], F32)
        rstd2 = sb("rstd2", [P, 2, 2], F32)
        xn2 = sb("xn2", [P, 2, 2, D], F32)
        xnT2 = sb("xnT2", [D, 2, L], F32)
        rc = sb("rc", [P, 2, 2 * D], F32)
        rs = sb("rs", [P, 2, 2 * D], F32)
        rot = sb("rot", [P, 2, 2 * D], F32)
        rem = sb("rem", [P, 2, 2 * D], F32)
        parts = [[sb(f"parts{u}{t}", [P, 2, H, KROWS], BF16) for t in range(2)] for u in range(2)]
        qT = [sb(f"qT{u}", [P, H // 2, L], BF16) for u in range(2)]
        kT = [sb(f"kT{u}", [P, H // 2, 2, L], BF16) for u in range(2)]
        vstage = sb("vstage", [P, 2, 2, D], F32)
        vx = [sb(f"vx{u}", [P, 2, H, 32], F32) for u in range(2)]
        negmax = sb("negmax", [P, 2, 2, H], F32)
        mrem = sb("mrem", [P, 2, H], F32)
        probs = sb("probs", [P, 8, 2 * L], F32)
        pvs = sb("pvs", [P, 2, L], F32)
        rden = sb("rden", [P, 16, 2], F32)
        oatt = sb("oatt", [P, 2, D], F32)
        oT = sb("oT", [D, L], F32)

        bank = [ctx.enter_context(nc.psum_tensor(f"bank{i}", [P, 512], F32)) for i in range(8)]
        work, sbank, stbank, pvbank = bank[0:2], bank[2:4], bank[4:6], bank[6:8]

        x_loaded = sems("x_loaded", CHUNKS)
        tab_loaded, shw_loaded, rw_loaded, aw_loaded = (sem(n) for n in ("tab_loaded", "shw_loaded", "rw_loaded", "aw_loaded"))
        consts_set, zeros_set, zeros_stored = sem("consts_set"), sem("zeros_set"), sem("zeros_stored")
        ln_stats, ln_rstd, xn_ready = sem("ln_stats"), sem("ln_rstd"), sem("xn_ready")
        xT_filled, xT_copied = sem("xT_filled"), sem("xT_copied")
        lgT_filled, lgT_copied, lg_filled, lg_copied = (sem(n) for n in ("lgT_filled", "lgT_copied", "lg_filled", "lg_copied"))
        top_ready, tanh_ready, score_ready, onehot_ready = (sem(n) for n in ("top_ready", "tanh_ready", "score_ready", "onehot_ready"))
        rank_filled, slot_ready, xs_ready, scattered = (sem(n) for n in ("rank_filled", "slot_ready", "xs_ready", "scattered"))
        expert_ready = sem("expert_ready")
        sg_filled, su_filled, ssilu, sh_ready, sy_filled, sy_added = (sem(n) for n in ("sg_filled", "su_filled", "ssilu", "sh_ready", "sy_filled", "sy_added"))
        xg_loaded = sems("xg_loaded", LOADS)
        xgs_ready = sem("xgs_ready")
        gT_filled, gT_copied, gu_filled, rsilu, rh_ready = (sem(n) for n in ("gT_filled", "gT_copied", "gu_filled", "rsilu", "rh_ready"))
        hT_filled, hT_copied, ry_filled, ys_ready, ys_stored = (sem(n) for n in ("hT_filled", "hT_copied", "ry_filled", "ys_ready", "ys_stored"))
        gathered = sems("gathered", TILES)
        ffn_added, out_stored = sem("ffn_added"), sem("out_stored")
        waited = sem("waited")
        dve_step, pool_step = sem("dve_step"), sem("pool_step")
        uses = ["q0", "k0", "q1", "k1", "back", "xT", "oT", "qkv0", "wo", "qkv1", "qm0", "qm1"]
        lag = dict(q0=1, k0=1, q1=1, k1=1, back=-1, xT=2, oT=-1, qkv0=2, wo=-1, qkv1=2, qm0=1, qm1=1)
        filled = {n: sem("filled_" + n) for n in uses}
        emptied = {n: sem("emptied_" + n) for n in uses}
        a_stats, a_rstd, a_xn = sem("a_stats"), sem("a_rstd"), sem("a_xn")
        roped, rotated, part1, rem_ready, part2, part3, vx_ready = (sem(n) for n in ("roped", "rotated", "part1", "rem_ready", "part2", "part3", "vx_ready"))
        s_filled, s_reduced, m_split = sem("s_filled"), sem("s_reduced"), sem("m_split")
        st_filled, exp_done, pv_done, pv_copied = sem("st_filled"), sem("exp_done"), sem("pv_done"), sem("pv_copied")
        o_ready = sem("o_ready")

        def wait_apart(eng, s, value):
            eng.wait_ge(s, value)
            if not isinstance(value, int):
                eng.sem_inc(waited, 1)

        class Steps:

            def __init__(self, eng, s):
                self.eng, self.s, self.n, self.moved = eng, s, 0, 0

            def link(self, ins):
                ins.then_inc(self.s, 1)
                self.n += 1
                wait_apart(self.eng, self.s, self.n + self.moved)

            def loop(self, i, start, step, body, per, turns):
                first = self.n
                self.moved = (i - start) * (per // step)
                body()
                assert self.n == first + per, self.n - first
                self.n, self.moved = first + per * turns, 0

        LOOP = (2, 6, 2)

        def attention(eng, turn, steps=None, per=0):
            def run(i, u):
                e, m, pr, f = 0 <= i < B, 0 <= i + 1 < B, 0 <= i + 2 < B, 0 <= i - 1 < B
                turn(i, u, e, m, pr, f)

            for i in range(-2, LOOP[0]):
                run(i, i % 2)
            with eng.Fori(LOOP[0] // LOOP[2], LOOP[1] // LOOP[2]) as w:
                i = w * LOOP[2]

                def body():
                    for k in range(LOOP[2]):
                        turn(i + k, (LOOP[0] + k) % 2, True, True, True, True)
                if steps is None:
                    body()
                else:
                    steps.loop(i, LOOP[0], LOOP[2], body, per, (LOOP[1] - LOOP[0]) // LOOP[2])
            for i in range(LOOP[1], B + 1):
                run(i, i % 2)

        RLOOP = (3, SLOT_TILES - 4 - (SLOT_TILES - 7) % 2, 2)

        def routed(eng, turn, first):
            def run(j):
                turn(j, j % 2, lambda k: 0 <= j + k < SLOT_TILES and j + k >= 0)
            for j in range(first, RLOOP[0]):
                run(j)
            with eng.Fori(*RLOOP) as j:
                for k in range(RLOOP[2]):
                    turn(j + k, (RLOOP[0] + k) % 2, lambda _: True)
            for j in range(RLOOP[1], SLOT_TILES + 1):
                run(j)

        block = ctx.enter_context(nc.Block())

        @block.sync
        def _(sp):
            xv = x_in.rearrange("(c i p) d -> c p i d", p=P, i=CHUNK)
            sp.dma_start(x[:, 0:CHUNK, :], xv[0]).then_inc(x_loaded[0], 16)
            sp.dma_start(tab[:], tab_in).then_inc(tab_loaded, 16)
            sp.dma_start(tabb[:], tabb_in).then_inc(tab_loaded, 16)
            for c in range(1, CHUNKS):
                sp.dma_start(x[:, c * CHUNK:(c + 1) * CHUNK, :], xv[c]).then_inc(x_loaded[c], 16)
            sp.dma_start(wgate[:], wgate_in).then_inc(shw_loaded, 16)
            sp.dma_start(shgu[:], shgu_in).then_inc(shw_loaded, 16)
            sp.dma_start(shdn[:], shdn_in).then_inc(shw_loaded, 16)
            sp.wait_ge(zeros_set, 1)
            sp.dma_start(xs_dram.rearrange("(j p) d -> p j d", p=P), xg[:, 0:SLOT_TILES, :]).then_inc(zeros_stored, 16)
            sp.dma_start(rgu[:], rgu_in).then_inc(rw_loaded, 16)
            sp.dma_start(rdn[:], rdn_in).then_inc(rw_loaded, 16)
            sp.dma_start(wqkv[:], wqkv_in).then_inc(aw_loaded, 16)
            sp.dma_start(wo[:], wo_in).then_inc(aw_loaded, 16)
            for n in range(2):
                sp.wait_ge(scattered, 16 * TILES * (n + 1))
                for k in range(LOADS):
                    j0, j1 = k * LOAD, min((k + 1) * LOAD, SLOT_TILES)
                    sp.dma_start(xg[:, j0:j1, :], xs_dram[j0 * P:j1 * P, :].rearrange("(j p) d -> p j d", p=P)).then_inc(xg_loaded[k], 16)
                with sp.Fori(0, SLOT_TILES) as j:
                    sp.wait_ge(ys_ready, j + (n * SLOT_TILES + 1))
                    sp.dma_start(ys_dram[bass.ts(j, P), :], ys[:, bass.ds(j, 1), :].rearrange("p a d -> p (a d)")).then_inc(ys_stored, 16)
            ov = out.rearrange("(c i p) d -> c p i d", p=P, i=CHUNK)
            for c in range(CHUNKS):
                sp.wait_ge(ffn_added, TILES + (c + 1) * CHUNK)
                sp.dma_start(ov[c], x[:, c * CHUNK:(c + 1) * CHUNK, :]).then_inc(out_stored, 16)
            sp.wait_ge(out_stored, 16 * CHUNKS)

        @block.gpsimd
        def _(pool):
            g = nc.gpsimd
            st = Steps(pool, pool_step)
            g.memset(neghalf[:], -0.5).then_inc(consts_set, 1)
            pool.wait_ge(consts_set, 1)

            def ffn_rstd(n):
                for c in range(CHUNKS):
                    pool.wait_ge(ln_stats, n * CHUNKS + c + 1)
                    s = slice(c * CHUNK, (c + 1) * CHUNK)
                    st.link(g.tensor_scalar_add(rstd[:, s], meanvar[:, s, 1], EPS))
                    g.tensor_tensor(rstd[:, s], rstd[:, s], neghalf[:, s], ALU.pow).then_inc(ln_rstd, 1)
                    if n == 0 and c == 1:
                        g.memset(xg[:], 0.0).then_inc(zeros_set, 1)

            def scatter(n):
                pool.wait_ge(slot_ready, n + 1)
                if n == 0:
                    pool.wait_ge(zeros_stored, 16)
                for i in range(TILES):
                    pool.wait_ge(xs_ready, n * TILES + i + 1)
                    g.indirect_dma_start(
                        xs_dram, bass.IndirectOffsetOnAxis(ap=slot[:, i:i + 1], axis=0), xs[:, i, :], None,
                        bounds_check=SLOT_TILES * P - 1, oob_is_err=False).then_inc(scattered, 16)

            def stage(n):
                r = n * SLOT_TILES
                for k in range(LOADS):
                    pool.wait_ge(xg_loaded[k], 16 * (n + 1))

                def one(j, u):
                    if not isinstance(j, int) or j >= 2 or n:
                        wait_apart(pool, gT_filled, j + (r - 1))
                    g.tensor_copy(xgs[:, u, :], xg[:, bass.ds(j, 1), :].rearrange("p a d -> p (a d)")).then_inc(xgs_ready, 1)

                one(0, 0)
                one(1, 1)
                with pool.Fori(2, SLOT_TILES - SLOT_TILES % 2, 2) as j:
                    one(j, 0)
                    one(j + 1, 1)
                if SLOT_TILES % 2:
                    one(SLOT_TILES - 1, 0)

            def gather(n):
                pool.wait_ge(ys_stored, 16 * SLOT_TILES * (n + 1))
                for i in range(TILES):
                    g.indirect_dma_start(
                        yg[:, i, :], None, ys_dram, bass.IndirectOffsetOnAxis(ap=slot[:, i:i + 1], axis=0),
                        bounds_check=SLOT_TILES * P - 1, oob_is_err=False).then_inc(gathered[i], 16)

            ffn_rstd(0)
            for u in range(2):
                g.memset(kT[u][:].bitcast(F32), 0.0).then_inc(consts_set, 1)
                g.memset(vx[u][:], 0.0).then_inc(consts_set, 1)
                for t in range(2):
                    g.memset(parts[u][t][:].bitcast(F32), 0.0).then_inc(consts_set, 1)
            pool.wait_ge(consts_set, 9)
            for u in range(2):
                v5 = vx[u][:].rearrange("p t (f s g) c -> p (t f) s g c", f=2, s=2)
                for s_ in range(2):
                    g.memset(v5[:, :, s_, :, 16 + s_:17 + s_], 1.0).then_inc(consts_set, 1)
                for t in range(2):
                    g.memset(parts[u][t][:, 1, :, MCOL:MCOL + 3], 1.0).then_inc(consts_set, 1)
            scatter(0)
            stage(0)
            gather(0)

            def turn(i, u, e, m, pr, f):
                if pr:
                    wait_apart(pool, a_stats, i + 3)
                    st.link(g.tensor_scalar_add(rstd2[:, u, :], meanvar2[:, u, :, 1], EPS))
                    g.tensor_tensor(rstd2[:, u, :], rstd2[:, u, :], neghalf[:, 0:2], ALU.pow).then_inc(a_rstd, 1)

                v = 1 - u

                def split_max(t):
                    wait_apart(pool, s_reduced, 16 * (i + 1) + 8 * t + 8)
                    mc = [parts[v][t][:, 0, :, MCOL + k] for k in range(3)]
                    st.link(g.tensor_copy(mc[0], negmax[:, v, t, :]))
                    st.link(g.tensor_tensor(mrem[:, t, :], negmax[:, v, t, :], mc[0], ALU.subtract))
                    st.link(g.tensor_copy(mc[1], mrem[:, t, :]))
                    g.tensor_tensor(mc[2], mrem[:, t, :], mc[1], ALU.subtract).then_inc(m_split, 1)

                if m:
                    wait_apart(pool, emptied["qkv1"], i + 2)
                    if not isinstance(i, int) or i >= 1:
                        wait_apart(pool, pv_done, 4 * i)
                    for t in range(2):
                        vs = vstage[:, v, t, :].rearrange("p (f s g d) -> p f s g d", f=2, s=2, g=4)
                        vd = vx[v][:, t].rearrange("p (f s g) c -> p f s g c", f=2, s=2)
                        for k in range(2):
                            ins = g.tensor_copy(vd[:, :, k, :, k * DH:(k + 1) * DH], vs[:, :, k])
                    ins.then_inc(vx_ready, 1)
                for t in range(2):
                    if m:
                        split_max(t)
                    if pr:
                        pt = parts[u][t]
                        if not isinstance(i, int) or i >= 0:
                            wait_apart(pool, filled["qm1"], i + 1)
                        g.memset(pt[:, 0, :, MCOL:MCOL + 3], 0.0)
                        wait_apart(pool, roped, 2 * (i + 2) + t + 1)
                        g.tensor_tensor(rot[:, t, :], rc[:, t, :], rs[:, t, :], ALU.add).then_inc(rotated, 1)
                        wait_apart(pool, part1, 2 * (i + 2) + t + 1)
                        r3 = lambda a: a[:, t, :].rearrange("p (q h d) -> p (q h) d", q=2, h=H)
                        flat = pt[:].rearrange("p q h c -> p (q h) c")
                        g.tensor_tensor(r3(rem), r3(rot), flat[:, :, 2 * DH:3 * DH], ALU.subtract).then_inc(rem_ready, 1)
                        wait_apart(pool, part2, 2 * (i + 2) + t + 1)
                        for q, at in ((0, 3), (1, 0)):
                            ins = g.tensor_tensor(
                                pt[:, q, :, at * DH:(at + 1) * DH], rem[:, t, q * D:(q + 1) * D].rearrange("p (h d) -> p h d", h=H),
                                pt[:, q, :, 5 * DH:6 * DH], ALU.subtract)
                        ins.then_inc(part3, 1)

            attention(pool, turn, st, 2 * (1 + 6))
            ffn_rstd(1)
            scatter(1)
            stage(1)
            gather(1)

        @block.scalar
        def _(act):
            a = nc.scalar

            def ffn(n):
                for c in range(CHUNKS):
                    act.wait_ge(xT_filled, n * CHUNKS + c + 1)
                    a.copy(xnT[:, c * 512:(c + 1) * 512], bank[c % 2][:]).then_inc(xT_copied, 1)

                def silu(c):
                    act.wait_ge(sg_filled, n * CHUNKS + c + 1)
                    if n * CHUNKS + c:
                        act.wait_ge(sh_ready, n * CHUNKS + c)
                    for k in range(2):
                        ins = a.activation(sgate[:, k, :], bank[2 + k][:], ACT.Silu)
                        ins.then_inc(ssilu, 1)

                silu(0)
                act.wait_ge(top_ready, n + 1)
                a.activation(tanh_half[:], top[:], ACT.Tanh, scale=0.5).then_inc(tanh_ready, 1)
                act.wait_ge(score_ready, n + 1)
                for i in range(TILES):
                    a.activation(xs[:, i, :], xn[:, i, :], ACT.Copy, scale=score[:, i:i + 1]).then_inc(xs_ready, 1)
                for c in range(1, CHUNKS):
                    silu(c)

                r = n * SLOT_TILES

                def copy_gT(j, u):
                    act.wait_ge(gT_filled, j + (r + 1))
                    a.copy(xgT[:, u, :], bank[u][:, 0:P]).then_inc(gT_copied, 1)

                def turn(j, u, has):
                    if has(1):
                        act.wait_ge(gu_filled, j + (r + 2))
                        if not isinstance(j, int) or j >= 1:
                            act.wait_ge(rh_ready, j + r)
                        a.activation(rsg[:, 1 - u, :], bank[3 - u][:, 0:F], ACT.Silu).then_inc(rsilu, 1)
                    if has(3):
                        copy_gT(j + 3, 1 - u)
                    if has(0):
                        act.wait_ge(hT_filled, j + (r + 1))
                        if not isinstance(j, int) or j >= 2 or n:
                            act.wait_ge(ry_filled, j + (r - 1))
                        a.copy(rhT[:, u, :, :].rearrange("p k s -> p (k s)"), bank[4 + u][:, 0:2 * P]).then_inc(hT_copied, 1)

                copy_gT(0, 0)
                copy_gT(1, 1)
                routed(act, turn, -1)

            def turn(i, u, e, m, pr, f):
                v = 1 - u
                for s_ in range(16):
                    if e:
                        h = s_
                        act.wait_ge(st_filled, 16 * i + h + 1)
                        if not isinstance(i, int) or 4 * i + h // 4 >= 2:
                            act.wait_ge(pv_done, 4 * i + (h // 4 - 1))
                        a.activation(probs[:, h % 8, :], stbank[h % 2][:], ACT.Exp, scale=float(DH) ** -0.5).then_inc(exp_done, 1)
                    if s_ == 0 and f:
                        act.wait_ge(pv_done, 4 * i)
                        a.copy(pvs[:].rearrange("p f s -> p (f s)"), pvbank[v][:]).then_inc(pv_copied, 1)
                    if s_ in (1, 3) and m:
                        t = s_ // 2
                        name = f"k{t}"
                        act.wait_ge(filled[name], i + 2)
                        src = work[uses.index(name) % 2][:].bitcast(BF16).rearrange("p (r s) -> p r s", r=8)
                        for k in range(2):
                            ins = a.copy(kT[v][64 * k:64 * k + 64, :, k, t * P:(t + 1) * P], src[64 * k:64 * k + 64])
                        ins.then_inc(emptied[name], 1)
                    if s_ == 6 and pr:
                        act.wait_ge(filled["xT"], i + 3)
                        a.copy(xnT2[:, u, :], work[1][:, 0:L]).then_inc(emptied["xT"], 1)
                    if s_ == 7 and f:
                        act.wait_ge(filled["oT"], i)
                        a.copy(oT[:], work[0][:, 0:L]).then_inc(emptied["oT"], 1)
                    if s_ in (10, 13) and pr:
                        t = int(s_ == 13)
                        pt = parts[u][t]
                        act.wait_ge(rotated, 2 * (i + 2) + t + 1)
                        if not isinstance(i, int) or i >= 0:
                            act.wait_ge(filled["qm1"], i + 1)
                        for q, at in ((0, slice(0, 6, 2)), (1, slice(1, 4))):
                            src = rot[:, t, q * D:(q + 1) * D].rearrange("p (h d) -> p h d", h=H)
                            dst = pt[:, q, :, 0:MCOL].rearrange("p h (s d) -> p h s d", s=6)[:, :, at, :]
                            ins = a.copy(dst, src.unsqueeze(2).to_broadcast([P, H, 3, DH]))
                        ins.then_inc(part1, 1)
                    if s_ in (11, 14) and pr:
                        t = int(s_ == 14)
                        pt = parts[u][t]
                        act.wait_ge(rem_ready, 2 * (i + 2) + t + 1)
                        for q, at in ((0, slice(1, 6, 4)), (1, slice(4, 6))):
                            src = rem[:, t, q * D:(q + 1) * D].rearrange("p (h d) -> p h d", h=H)
                            dst = pt[:, q, :, 0:MCOL].rearrange("p h (s d) -> p h s d", s=6)[:, :, at, :]
                            ins = a.copy(dst, src.unsqueeze(2).to_broadcast([P, H, 2, DH]))
                        ins.then_inc(part2, 1)

            ffn(0)
            attention(act, turn)
            ffn(1)

        @block.vector
        def _(dve):
            v_ = nc.vector
            st = Steps(dve, dve_step)

            def normalise(o_, x_, mv, r_):
                return v_.tensor_scalar(o_, x_, mv, r_, ALU.subtract, ALU.mult)

            def ffn(n):
                def ln(c):
                    dve.wait_ge(ln_rstd, n * CHUNKS + c + 1)
                    for i in range(c * CHUNK, (c + 1) * CHUNK):
                        ins = normalise(xn[:, i, :], x[:, i, :], meanvar[:, i, 0:1], rstd[:, i:i + 1])
                        ins.then_inc(xn_ready, 1)

                for c in range(CHUNKS):
                    if n == 0:
                        dve.wait_ge(x_loaded[c], 16)
                    else:
                        dve.wait_ge(emptied["wo"], 2 * c + 2)
                    for i in range(c * CHUNK, (c + 1) * CHUNK):
                        ins = v_.bn_stats(stats[:, i, :], x[:, i, :])
                    st.link(ins)
                    for i in range(c * CHUNK, (c + 1) * CHUNK):
                        ins = v_.bn_aggr(meanvar[:, i, :], stats[:, i, :])
                    ins.then_inc(ln_stats, 1)
                    if c:
                        ln(c - 1)
                ln(CHUNKS - 1)

                dve.wait_ge(lgT_filled, n + 1)
                v_.tensor_copy(lgT[:], bank[7][:]).then_inc(lgT_copied, 1)
                dve.wait_ge(lg_filled, n + 1)
                src = bank[0][:].rearrange("p (c g k) -> p g c k", c=4, g=4)[:, :, :, 0:E]
                st.link(v_.tensor_copy(lg[:].rearrange("p (g c) e -> p g c e", g=4), src))
                lg_all = lambda a_: a_[:].unsqueeze(2).to_broadcast([P, TILES, E])
                v_.tensor_reduce(top[:], lg[:], AX.X, ALU.max).then_inc(top_ready, 1)
                dve.wait_ge(top_ready, n + 1)
                st.link(v_.tensor_tensor(is_top[:], lg[:], lg_all(top), ALU.is_equal))
                em8 = eminus8.unsqueeze(1).to_broadcast([P, TILES, E])
                st.link(v_.tensor_tensor(is_top[:], is_top[:], em8, ALU.mult))
                st.link(v_.tensor_reduce(first_top[:], is_top[:], AX.X, ALU.min))
                st.link(v_.tensor_tensor(onehot[:], em8, lg_all(first_top), ALU.is_equal))
                v_.tensor_copy(onehotb[:], onehot[:]).then_inc(onehot_ready, 1)
                dve.wait_ge(tanh_ready, n + 1)
                v_.tensor_scalar(score[:], tanh_half[:], 0.5, 0.5, ALU.mult, ALU.add).then_inc(score_ready, 1)

                def shared_hidden(c):
                    k0 = n * CHUNKS + c
                    dve.wait_ge(ssilu, 2 * k0 + 2)
                    dve.wait_ge(su_filled, k0 + 1)
                    if k0 >= 2:
                        dve.wait_ge(sy_filled, k0 - 1)
                    st.link(v_.tensor_tensor(sh[:, c % 2, 0, :], sgate[:, 0, :], bank[4][:], ALU.mult))
                    v_.tensor_tensor(sh[:, c % 2, 1, :], sgate[:, 1, :], bank[5][:], ALU.mult).then_inc(sh_ready, 1)

                def shared_add(c):
                    dve.wait_ge(sy_filled, n * CHUNKS + c + 1)
                    s = slice(c * CHUNK, (c + 1) * CHUNK)
                    xc = x[:, s, :].rearrange("p i d -> p (i d)")
                    v_.scalar_tensor_tensor(out=xc, in0=bank[6][:], scalar=0.5, in1=xc, op0=ALU.mult, op1=ALU.add).then_inc(sy_added, 1)

                dve.wait_ge(rank_filled, n + 1)
                rank = bank[7][:, 0:(TILES + 1) * E].rearrange("p (i e) -> p i e", e=E)
                st.link(v_.tensor_copy(total[:], rank[:, TILES, :]))
                st.link(v_.tensor_tensor(over[:], total[:].unsqueeze(2).to_broadcast([P, E, 16]),
                                         steps128.unsqueeze(1).to_broadcast([P, E, 16]), ALU.is_gt))
                st.link(v_.tensor_reduce(etiles[:], over[:], AX.X, ALU.add))
                st.link(v_.tensor_tensor(etb[:], before, etiles[:].unsqueeze(1).to_broadcast([P, E, E]), ALU.mult))
                st.link(v_.tensor_reduce(estart[:], etb[:], AX.X, ALU.add))
                st.link(v_.tensor_scalar(estart128[:], estart[:], float(P), None, ALU.mult))
                st.link(v_.tensor_tensor(slot8[:], rank[:, 0:TILES, :], estart128[:].unsqueeze(1).to_broadcast([P, TILES, E]), ALU.add))
                st.link(v_.tensor_tensor(slot8[:], slot8[:], onehot[:], ALU.mult))
                st.link(v_.tensor_reduce(slotf[:], slot8[:], AX.X, ALU.add))
                v_.tensor_copy(slot[:], slotf[:]).then_inc(slot_ready, 1)
                st.link(v_.tensor_tensor(eend[:], estart[:], etiles[:], ALU.add))
                st.link(v_.tensor_tensor(ended[:], eend[0:1, :].unsqueeze(1).to_broadcast([1, SLOT_TILES, E]),
                                         tile_no[0:1, :].unsqueeze(2).to_broadcast([1, SLOT_TILES, E]), ALU.is_le))
                st.link(v_.tensor_reduce(expertf[:], ended[:], AX.X, ALU.add))
                st.link(v_.tensor_scalar(expertf[:], expertf[:], float(E - 1), None, ALU.min))
                v_.tensor_copy(expert[:], expertf[:]).then_inc(expert_ready, 1)

                shared_hidden(0)
                for c in range(1, CHUNKS):
                    shared_hidden(c)
                    shared_add(c - 1)
                shared_add(CHUNKS - 1)

                r = n * SLOT_TILES

                def turn(j, u, has):
                    if has(1):
                        dve.wait_ge(rsilu, j + (r + 2))
                        if not isinstance(j, int) or j >= 1 or n:
                            dve.wait_ge(hT_filled, j + r)
                        v_.tensor_tensor(rh[:, 1 - u, :], rsg[:, 1 - u, :], bank[3 - u][:, F:2 * F], ALU.mult).then_inc(rh_ready, 1)
                    if has(-1):
                        dve.wait_ge(ry_filled, j + r)
                        v_.tensor_copy(ys[:, bass.ds(j - 1, 1), :].rearrange("p a d -> p (a d)"), bank[6 + (1 - u)][:, 0:D]).then_inc(ys_ready, 1)

                routed(dve, turn, -1)
                if n:
                    add_experts(n, 0, TILES)

            def add_experts(n, i0, i1):
                if i0 == 0:
                    dve.wait_ge(sy_added, CHUNKS * (n + 1))
                for i in range(i0, i1):
                    dve.wait_ge(gathered[i], 16 * (n + 1))
                    v_.scalar_tensor_tensor(out=x[:, i, :], in0=yg[:, i, :], scalar=0.5, in1=x[:, i, :], op0=ALU.mult, op1=ALU.add).then_inc(ffn_added, 1)

            def turn(i, u, e, m, pr, f):
                v = 1 - u

                def q_copy(name, t):
                    dve.wait_ge(filled[name], i + 2)
                    v_.tensor_copy(qT[v][:, :, t * P:(t + 1) * P],
                                   work[uses.index(name) % 2][:].bitcast(BF16).rearrange("p (r s) -> p r s", r=8)).then_inc(emptied[name], 1)

                def reduce(k):
                    dve.wait_ge(s_filled, 16 * (i + 1) + k + 1)
                    t, pair = k // 8, k % 8
                    v_.tensor_reduce(negmax[:, v, t, 2 * pair:2 * pair + 2], sbank[k % 2][:].rearrange("p (a s) -> p a s", a=2),
                                     AX.X, ALU.max, negate=True).then_inc(s_reduced, 1)

                def rope(t):
                    name = f"qkv{t}"
                    dve.wait_ge(filled[name], i + 3)
                    if not isinstance(i, int) or i >= -1:
                        dve.wait_ge(rotated, 2 * (i + 1) + t + 1)
                    bk = work[1]
                    qk = bk[:, 0:2 * D]
                    pairs = qk.rearrange("p (r two) -> p r two", two=2)
                    sp_, sn = rs[:, t, :].rearrange("p (r two) -> p r two", two=2), sin[:, t, :].rearrange("p (r two) -> p r two", two=2)
                    v_.tensor_tensor(rc[:, t, :], qk, cos[:, t, :], ALU.mult)
                    v_.tensor_tensor(sp_[:, :, 0], pairs[:, :, 1], sn[:, :, 0], ALU.mult)
                    v_.tensor_tensor(sp_[:, :, 1], pairs[:, :, 0], sn[:, :, 1], ALU.mult).then_inc(roped, 1)
                    if not isinstance(i, int) or i >= 0:
                        dve.wait_ge(vx_ready, i + 1)
                    v_.tensor_copy(vstage[:, u, t, :], bk[:, 2 * D:3 * D]).then_inc(emptied[name], 1)

                if isinstance(i, int) and i < 1:
                    add_experts(0, *((0, 4), (4, 10), (10, 16))[i + 2])
                k = 0
                for s_ in range(16):
                    if s_ in (0, 2) and m:
                        q_copy(f"q{s_ // 2}", s_ // 2)
                    if s_ == 3 and pr:
                        dve.wait_ge(ffn_added, 2 * (i + 2) + 2)
                        for t in range(2):
                            ins = v_.bn_stats(stats2[:, t, :], x[:, bass.ds(2 * (i + 2) + t, 1), :].rearrange("p a d -> p (a d)"))
                        st.link(ins)
                        for t in range(2):
                            ins = v_.bn_aggr(meanvar2[:, u, t, :], stats2[:, t, :])
                        ins.then_inc(a_stats, 1)
                    if m and s_ >= 4:
                        n_ = (s_ - 3) * 4 // 3
                        while k < n_:
                            reduce(k)
                            k += 1
                    if s_ == 4 and pr:
                        dve.wait_ge(a_rstd, i + 3)
                        for t in range(2):
                            ins = normalise(xn2[:, u, t, :], x[:, bass.ds(2 * (i + 2) + t, 1), :].rearrange("p a d -> p (a d)"),
                                            meanvar2[:, u, t, 0:1], rstd2[:, u, t:t + 1])
                            ins.then_inc(a_xn, 1)
                    if s_ == 4 and f:
                        dve.wait_ge(filled["back"], i)
                        bk = work[0][:].rearrange("p (x g c) -> p x g c", x=4, g=4)
                        st.link(v_.reciprocal(rden[:], work[0][:].rearrange("p (x c) -> p x c", x=16)[:, :, 16:18]))
                        ov = oatt[:].rearrange("p t (f s g d) -> p (t f) s g d", f=2, s=2, g=4)
                        rv = rden[:].rearrange("p (x g) s -> p x g s", x=4)
                        for s2 in range(2):
                            ins = v_.tensor_tensor(ov[:, :, s2], bk[:, :, :, s2 * DH:(s2 + 1) * DH],
                                                   rv[:, :, :, s2].unsqueeze(3).to_broadcast([P, 4, 4, DH]), ALU.mult)
                        ins.then_inc(emptied["back"], 1)
                    if s_ == 9 and f:
                        dve.wait_ge(filled["wo"], i)
                        xb = x[:, bass.ds(2 * (i - 1), 2), :].rearrange("p t d -> p (t d)")
                        v_.tensor_tensor(xb, work[0][:, 0:L], xb, ALU.add).then_inc(emptied["wo"], 1)
                    if s_ in (8, 11) and pr:
                        rope(int(s_ == 11))
                    if s_ == 11 and m:
                        q_copy("qm0", 0)
                if m:
                    q_copy("qm1", 1)

            ffn(0)
            attention(dve, turn, st, 2 * 2)
            ffn(1)

        @block.tensor
        def _(pe):
            t_ = nc.tensor

            def mm(o_, l, r, start=True, stop=True, **k):
                return t_.matmul(o_, l, r, start=start, stop=stop, **k)

            def ffn(n):
                if n == 0:
                    pe.wait_ge(tab_loaded, 32)
                else:
                    pe.wait_ge(emptied["wo"], B)
                    pe.wait_ge(exp_done, 16 * B)
                for c in range(CHUNKS):
                    pe.wait_ge(xn_ready, (n * CHUNKS + c + 1) * CHUNK)
                    if c >= 2:
                        pe.wait_ge(xT_copied, n * CHUNKS + c - 1)
                    for i in range(CHUNK):
                        ins = t_.transpose(bank[c % 2][:, i * P:(i + 1) * P], xn[:, c * CHUNK + i, :], ident)
                    ins.then_inc(xT_filled, 1)
                if n == 0:
                    pe.wait_ge(shw_loaded, 48)
                for c in range(CHUNKS):
                    pe.wait_ge(xT_copied, n * CHUNKS + c + 1)
                    ins = mm(bank[7][32 * c:32 * c + 32, :], wgate[:], xnT[:, c * 512:(c + 1) * 512])
                ins.then_inc(lgT_filled, 1)

                def shared_gate(c):
                    k0 = n * CHUNKS + c
                    if k0:
                        pe.wait_ge(ssilu, 2 * k0)
                    for k in range(2):
                        ins = mm(bank[2 + k][:], shgu[:, k * P:(k + 1) * P], xnT[:, c * 512:(c + 1) * 512])
                    ins.then_inc(sg_filled, 1)

                def shared_up(c):
                    k0 = n * CHUNKS + c
                    if k0:
                        pe.wait_ge(sh_ready, k0)
                    for k in range(2):
                        ins = mm(bank[4 + k][:], shgu[:, F + k * P:F + (k + 1) * P], xnT[:, c * 512:(c + 1) * 512])
                    ins.then_inc(su_filled, 1)

                def shared_down(c):
                    k0 = n * CHUNKS + c
                    pe.wait_ge(sh_ready, k0 + 1)
                    if k0:
                        pe.wait_ge(sy_added, k0)
                    for i in range(CHUNK):
                        for k in range(2):
                            ins = mm(bank[6][:, i * P:(i + 1) * P], sh[:, c % 2, k, i * P:(i + 1) * P], shdn[:, k, :],
                                     start=(k == 0), stop=(k == 1))
                    ins.then_inc(sy_filled, 1)

                shared_gate(0)
                pe.wait_ge(lgT_copied, n + 1)
                for c in range(4):
                    ins = t_.transpose(bank[0][:, c * P:(c + 1) * P], lgT[:, c * P:(c + 1) * P], ident)
                ins.then_inc(lg_filled, 1)
                shared_up(0)
                pe.wait_ge(onehot_ready, n + 1)
                rank = bank[7][:, 0:(TILES + 1) * E]
                oh = onehotb[:]
                mm(rank[:, 0:TILES * E], upper, oh.rearrange("p i e -> p (i e)"), stop=False, skip_group_check=True)
                for i in range(TILES):
                    w = TILES - i
                    ins = mm(rank[:, (i + 1) * E:].rearrange("p (i e) -> p i e", e=E), onesb,
                             oh[:, i:i + 1, :].to_broadcast([P, w, E]), start=False, stop=(i == TILES - 1), skip_group_check=True)
                ins.then_inc(rank_filled, 1)
                for c in range(1, CHUNKS):
                    shared_gate(c)
                    shared_down(c - 1)
                    shared_up(c)
                shared_down(CHUNKS - 1)

                r = n * SLOT_TILES
                if n == 0:
                    pe.wait_ge(rw_loaded, 32)
                pe.wait_ge(expert_ready, n + 1)

                def turn_g(j, u):
                    pe.wait_ge(xgs_ready, j + (r + 1))
                    if not isinstance(j, int) or j >= 2:
                        pe.wait_ge(gT_copied, j + (r - 1))
                    t_.transpose(bank[u][:, 0:P], xgs[:, u, :], ident).then_inc(gT_filled, 1)

                def turn(j, u, has):
                    if has(1):
                        ex = t_.value_load(expert[0:1, bass.ds(j + 1, 1)], min_val=0, max_val=E - 1)
                        pe.wait_ge(gT_copied, j + (r + 2))
                        if not isinstance(j, int) or j >= 1 or n:
                            pe.wait_ge(rh_ready, j + r)
                        mm(bank[3 - u][:], xgT[:, 1 - u, :], rgu[:, bass.ds(ex * (2 * F), 2 * F)]).then_inc(gu_filled, 1)
                    if has(3):
                        turn_g(j + 3, 1 - u)
                    if has(0):
                        pe.wait_ge(rh_ready, j + (r + 1))
                        for k in range(2):
                            ins = t_.transpose(bank[4 + u][:, k * P:(k + 1) * P], rh[:, u, k * P:(k + 1) * P], ident)
                        ins.then_inc(hT_filled, 1)
                    if has(-1):
                        v = 1 - u
                        ex = t_.value_load(expert[0:1, bass.ds(j - 1, 1)], min_val=0, max_val=E - 1)
                        pe.wait_ge(hT_copied, j + r)
                        if not isinstance(j, int) or j >= 3:
                            pe.wait_ge(ys_ready, j + (r - 2))
                        for k in range(2):
                            ins = mm(bank[6 + v][:, 0:D], rhT[:, v, k, :], rdn[:, bass.ds(ex * (2 * D) + k * D, D)], start=(k == 0), stop=(k == 1))
                        ins.then_inc(ry_filled, 1)

                turn_g(0, 0)
                turn_g(1, 1)
                routed(pe, turn, -1)

            def turn(i, u, e, m, pr, f):
                v = 1 - u
                static = isinstance(i, int)

                def work_bank(name):
                    at = uses.index(name)
                    back = 0
                    while True:
                        back += 2
                        before_ = uses[(at - back) % len(uses)]
                        turns = (back - at + len(uses) - 1) // len(uses) if back > at else 0
                        seq = i - turns + lag[before_]
                        if not static or 0 <= seq < B:
                            pe.wait_ge(emptied[before_], seq + 1)
                            break
                        if back > 4 * len(uses):
                            break
                    return work[at % 2]

                def parts_turned(name, t, q):
                    w = work_bank(name)[:].bitcast(BF16)
                    for k in range(H // 2):
                        ins = t_.transpose(w[:, k * P:(k + 1) * P],
                                           parts[v][t][:, q, 2 * k:2 * k + 2, :].rearrange("p a c -> p (a c)"), identb)
                    ins.then_inc(filled[name], 1)

                def scores(k):
                    t, pair = k // 8, k % 8
                    if k == 0:
                        for name in ("q0", "k0", "k1"):
                            pe.wait_ge(emptied[name], i + 2)
                    if k == 8:
                        pe.wait_ge(emptied["q1"], i + 2)
                    if not static or 16 * (i + 1) + k >= 2:
                        pe.wait_ge(s_reduced, 16 * (i + 1) + (k - 1))
                    mm(sbank[k % 2][:], qT[v][:, pair, t * P:(t + 1) * P],
                       kT[v][:, pair, :, :].rearrange("p a s -> p (a s)")).then_inc(s_filled, 1)

                def scores_t(h):
                    if h == 0:
                        for name in ("qm0", "qm1"):
                            pe.wait_ge(emptied[name], i + 1)
                    if not static or 16 * i + h >= 2:
                        pe.wait_ge(exp_done, 16 * i + (h - 1))
                    for k in range(2):
                        ins = mm(stbank[h % 2][:, k * L:(k + 1) * L], kT[u][:, h // 2, h % 2, k * P:(k + 1) * P], qT[u][:, h // 2, :])
                    ins.then_inc(st_filled, 1)

                def values(k):
                    if k == 0:
                        pe.wait_ge(vx_ready, i + 1)
                        if not static or i >= 2:
                            pe.wait_ge(pv_copied, i - 1)
                    pe.wait_ge(exp_done, 16 * i + 4 * k + 4)
                    half, sub = k // 2, k % 2
                    for c in range(2):
                        for g in range(4):
                            h = 4 * k + g
                            first = sub == 0 and c == 0
                            ins = mm(pvbank[u][32 * g:32 * g + 32, half * L:(half + 1) * L], vx[u][:, c, h, :],
                                     probs[:, h % 8, c * L:(c + 1) * L], start=first, stop=(sub == 1 and c == 1))
                    ins.then_inc(pv_done, 1)

                k = 0
                for s_ in range(16):
                    if e:
                        scores_t(s_)
                    if m and s_ < 4:
                        t, q = s_ // 2, s_ % 2
                        if s_ == 0:
                            pe.wait_ge(part3, 2 * (i + 1) + 2)
                        parts_turned("qk"[q] + str(t), t, q)
                    if e and s_ in (5, 9, 13):
                        values(s_ // 4 - 1)
                    if s_ == 4 and f:
                        w = work_bank("back")
                        pe.wait_ge(pv_copied, i)
                        for c in range(4):
                            ins = t_.transpose(w[:, c * P:(c + 1) * P], pvs[:, c % 2, (c // 2) * P:(c // 2 + 1) * P], ident)
                        ins.then_inc(filled["back"], 1)
                    if s_ == 6 and pr:
                        w = work_bank("xT")
                        pe.wait_ge(a_xn, 2 * (i + 2) + 2)
                        for t in range(2):
                            ins = t_.transpose(w[:, t * P:(t + 1) * P], xn2[:, u, t, :], ident)
                        ins.then_inc(filled["xT"], 1)
                    if s_ == 7 and f:
                        w = work_bank("oT")
                        pe.wait_ge(emptied["back"], i)
                        for t in range(2):
                            ins = t_.transpose(w[:, t * P:(t + 1) * P], oatt[:, t, :], ident)
                        ins.then_inc(filled["oT"], 1)
                    if s_ in (8, 10) and pr:
                        t = int(s_ == 10)
                        w = work_bank(f"qkv{t}")
                        if t == 0:
                            pe.wait_ge(emptied["xT"], i + 3)
                        mm(w[:, 0:3 * D], xnT2[:, u, t * P:(t + 1) * P], wqkv[:]).then_inc(filled[f"qkv{t}"], 1)
                    if s_ == 9 and f:
                        w = work_bank("wo")
                        pe.wait_ge(emptied["oT"], i)
                        for t in range(2):
                            ins = mm(w[:, t * P:(t + 1) * P], oT[:, t * P:(t + 1) * P], wo[:])
                        ins.then_inc(filled["wo"], 1)
                    if m and s_ >= 4:
                        while k < (s_ - 3) * 4 // 3:
                            scores(k)
                            k += 1
                    if s_ == 11 and m:
                        pe.wait_ge(m_split, 2 * (i + 1) + 1)
                        parts_turned("qm0", 0, 0)
                if e:
                    values(3)
                if m:
                    pe.wait_ge(m_split, 2 * (i + 1) + 2)
                    parts_turned("qm1", 1, 0)

            ffn(0)
            pe.wait_ge(aw_loaded, 32)
            for s_ in (gT_copied, rh_ready, hT_copied, ys_ready):
                pe.wait_ge(s_, SLOT_TILES)
            attention(pe, turn)
            ffn(1)


TAB_COLS = P + 1024 + 88 + SLOT_TILES
TABB_COLS = 3 * P


def tables():
    f = np.float32
    freqs = np.exp((-np.log(10000.0)).astype(f) * np.arange(0, DH, 2, dtype=f) / f(DH)).astype(f)
    angle = (np.arange(L, dtype=f)[:, None] * freqs).astype(f)
    cos = np.tile(np.repeat(np.cos(angle), 2, axis=1), (1, 2 * H)).reshape(2, P, 2 * D).transpose(1, 0, 2).reshape(P, 4 * D)
    signed = np.stack([-np.sin(angle), np.sin(angle)], axis=-1).reshape(L, DH)
    sin = np.tile(signed, (1, 2 * H)).reshape(2, P, 2 * D).transpose(1, 0, 2).reshape(P, 4 * D)
    row = lambda a: np.tile(np.asarray(a, f).reshape(1, -1), (P, 1))
    tab = np.concatenate([np.eye(P, dtype=f), cos, sin, row(np.arange(16) * P), row(np.tril(np.ones((E, E)), -1)),
                          row(np.arange(E) - E), row(np.arange(SLOT_TILES))], axis=1)
    tabb = np.concatenate([np.eye(P), np.triu(np.ones((P, P)), 1), np.ones((P, P))], axis=1)
    return np.ascontiguousarray(tab, f), tabb


def kernel(L0_attn_x, L0_attn_W_q, L0_attn_W_k, L0_attn_W_v, L0_attn_W_o, L0_ffn_gate_w, L0_ffn_shared_gate,
           L0_ffn_shared_up, L0_ffn_shared_down, L0_ffn_r_gate, L0_ffn_r_up, L0_ffn_r_down):
    import ml_dtypes
    import concourse.bacc as bacc
    from concourse.bass_utils import run_bass_kernel_spmd as run

    tab, tabb = tables()
    gate = np.zeros((D, 32), np.float32)
    gate[:, 0:E] = np.transpose(L0_ffn_gate_w)
    cols = lambda *a: np.concatenate([np.transpose(w) for w in a], axis=1)
    two = np.concatenate([np.transpose(L0_ffn_r_gate, (2, 0, 1)), np.transpose(L0_ffn_r_up, (2, 0, 1))], axis=2)
    arrays = {
        "x": np.reshape(L0_attn_x, (N, D)),
        "wqkv": cols(L0_attn_W_q, L0_attn_W_k, L0_attn_W_v),
        "wo": np.transpose(L0_attn_W_o),
        "wgate": gate,
        "shgu": cols(L0_ffn_shared_gate, L0_ffn_shared_up),
        "shdn": np.transpose(np.reshape(np.transpose(L0_ffn_shared_down), (2, P, D)), (1, 0, 2)),
        "rgu": np.reshape(two, (D, E * 2 * F)),
        "rdn": np.reshape(np.transpose(np.reshape(L0_ffn_r_down, (E, D, 2, P)), (3, 0, 2, 1)), (P, E * 2 * D)),
        "tab": tab,
        "tabb": tabb.astype(ml_dtypes.bfloat16),
    }
    arrays = {k: np.ascontiguousarray(v) for k, v in arrays.items()}
    nc = bacc.Bacc("TRN2", target_bir_lowering=False, num_devices=1)
    aps = [nc.dram_tensor("in_" + k, v.shape, mybir.dt.from_np(v.dtype), kind="ExternalInput").ap() for k, v in arrays.items()]
    out = nc.dram_tensor("out_x", (N, D), F32, kind="ExternalOutput").ap()
    build(nc, *aps, out)
    r = run(nc, [{"in_" + k: v for k, v in arrays.items()}], core_ids=[0])
    return np.reshape(r.results[0]["out_x"], (B, L, D))
```

```python
from contextlib import ExitStack

import concourse.bass as bass
from concourse import mybir
from concourse.alu_op_type import AluOpType as ALU
import numpy as np

ACT = mybir.ActivationFunctionType
AX = mybir.AxisListType
F32 = mybir.dt.float32
BF16 = mybir.dt.bfloat16
I32 = mybir.dt.int32
U32 = mybir.dt.uint32

P = 128
D = 128
B, L = 8, 256
H, DH = 16, 8
F = 256
E = 8
N = B * L
TILES = N // P
CHUNK = 4
CHUNKS = TILES // CHUNK
SLOT_TILES = TILES + E - 1
LOAD = 4
LOADS = -(-SLOT_TILES // LOAD)
EPS = 1e-5
KROWS = 64
MCOL = 6 * DH
QUADS = H // 4


def build(nc, x_in, wqkv_in, wo_in, wgate_in, shgu_in, shdn_in, rgu_in, rdn_in, tab_in, tabb_in, out):
    ctx = ExitStack()
    with ctx:
        def sb(name, shape, dt):
            return ctx.enter_context(nc.sbuf_tensor(name, shape, dt))

        def sem(name):
            return ctx.enter_context(nc.semaphore(name))

        def sems(name, n):
            return [sem(f"{name}{i}") for i in range(n)]

        x = sb("x", [P, TILES, D], F32)
        wqkv = sb("wqkv", [D, 3 * D], F32)
        wo = sb("wo", [D, D], F32)
        wgate = sb("wgate", [D, 32], F32)
        shgu = sb("shgu", [D, 2 * F], F32)
        shdn = sb("shdn", [P, 2, D], F32)
        rgu = sb("rgu", [D, E * 2 * F], F32)
        rdn = sb("rdn", [P, E * 2 * D], F32)
        tab = sb("tab", [P, TAB_COLS], F32)
        tabb = sb("tabb", [P, TABB_COLS], BF16)
        ident = tab[:, 0:P]
        cos = tab[:, P:P + 512].rearrange("p (t n) -> p t n", t=2)
        sin = tab[:, P + 512:P + 1024].rearrange("p (t n) -> p t n", t=2)
        o = P + 1024
        steps128 = tab[:, o:o + 16]
        before = tab[:, o + 16:o + 80].rearrange("p (e f) -> p e f", e=E)
        eminus8 = tab[:, o + 80:o + 88]
        tile_no = tab[:, o + 88:o + 88 + SLOT_TILES]
        identb = tabb[:, 0:P]
        upper = tabb[:, P:2 * P]
        onesb = tabb[:, 2 * P:3 * P]

        stats = sb("stats", [P, TILES, 6], F32)
        meanvar = sb("meanvar", [P, TILES, 2], F32)
        rstd = sb("rstd", [P, TILES], F32)
        neghalf = sb("neghalf", [P, TILES], F32)
        xn = sb("xn", [P, TILES, D], F32)
        xnT = sb("xnT", [D, N], F32)
        lgT = sb("lgT", [P, 512], F32)
        lg = sb("lg", [P, TILES, E], F32)
        top = sb("top", [P, TILES], F32)
        is_top = sb("is_top", [P, TILES, E], F32)
        first_top = sb("first_top", [P, TILES], F32)
        onehot = sb("onehot", [P, TILES, E], F32)
        onehotb = sb("onehotb", [P, TILES, E], BF16)
        tanh_half = sb("tanh_half", [P, TILES], F32)
        score = sb("score", [P, TILES], F32)
        total = sb("total", [P, E], F32)
        over = sb("over", [P, E, 16], F32)
        etiles = sb("etiles", [P, E], F32)
        etb = sb("etb", [P, E, E], F32)
        estart = sb("estart", [P, E], F32)
        estart128 = sb("estart128", [P, E], F32)
        eend = sb("eend", [P, E], F32)
        slot8 = sb("slot8", [P, TILES, E], F32)
        slotf = sb("slotf", [P, TILES], F32)
        slot = sb("slot", [P, TILES], U32)
        ended = sb("ended", [1, SLOT_TILES, E], F32)
        expertf = sb("expertf", [1, SLOT_TILES], F32)
        expert = sb("expert", [1, SLOT_TILES], I32)
        xs = sb("xs", [P, TILES, D], F32)
        sgate = sb("sgate", [P, 2, 512], F32)
        sh = sb("sh", [P, 2, 2, 512], F32)
        xg = sb("xg", [P, LOADS * LOAD, D], F32)
        xgs = sb("xgs", [P, 2, D], F32)
        xgT = sb("xgT", [P, 2, P], F32)
        rsg = sb("rsg", [P, 2, F], F32)
        rh = sb("rh", [P, 2, F], F32)
        rhT = sb("rhT", [P, 2, 2, P], F32)
        ys = sb("ys", [P, SLOT_TILES, D], F32)
        yg = xs
        xs_dram = nc.dram_tensor("xs_sorted", (SLOT_TILES * P, D), F32, kind="Internal").ap()
        ys_dram = nc.dram_tensor("ys_sorted", (SLOT_TILES * P, D), F32, kind="Internal").ap()

        stats2 = sb("stats2", [P, 2, 6], F32)
        meanvar2 = sb("meanvar2", [P, 2, 2, 2], F32)
        rstd2 = sb("rstd2", [P, 2, 2], F32)
        xn2 = sb("xn2", [P, 2, 2, D], F32)
        xnT2 = sb("xnT2", [D, 2, L], F32)
        rc = sb("rc", [P, 2, 2 * D], F32)
        rs = sb("rs", [P, 2, 2 * D], F32)
        rot = sb("rot", [P, 2, 2 * D], F32)
        rem = sb("rem", [P, 2, 2 * D], F32)
        parts = [[sb(f"parts{u}{t}", [P, 2, H, KROWS], BF16) for t in range(2)] for u in range(2)]
        qT = [sb(f"qT{u}", [P, H // 2, L], BF16) for u in range(2)]
        kT = [sb(f"kT{u}", [P, H // 2, 2, L], BF16) for u in range(2)]
        vstage = sb("vstage", [P, 2, 2, D], F32)
        vx = [sb(f"vx{u}", [P, 2, H, 32], F32) for u in range(2)]
        negmax = sb("negmax", [P, 2, 2, H], F32)
        mrem = sb("mrem", [P, 2, H], F32)
        probs = sb("probs", [P, 8, 2 * L], F32)
        pvs = sb("pvs", [P, 2, L], F32)
        rden = sb("rden", [P, 16, 2], F32)
        oatt = sb("oatt", [P, 2, D], F32)
        oT = sb("oT", [D, L], F32)

        bank = [ctx.enter_context(nc.psum_tensor(f"bank{i}", [P, 512], F32)) for i in range(8)]
        work, sbank, stbank, pvbank = bank[0:2], bank[2:4], bank[4:6], bank[6:8]

        x_loaded = sems("x_loaded", CHUNKS)
        tab_loaded, shw_loaded, rw_loaded, aw_loaded = (sem(n) for n in ("tab_loaded", "shw_loaded", "rw_loaded", "aw_loaded"))
        consts_set, zeros_set, zeros_stored = sem("consts_set"), sem("zeros_set"), sem("zeros_stored")
        ln_stats, ln_rstd, xn_ready = sem("ln_stats"), sem("ln_rstd"), sem("xn_ready")
        xT_filled, xT_copied = sem("xT_filled"), sem("xT_copied")
        lgT_filled, lgT_copied, lg_filled, lg_copied = (sem(n) for n in ("lgT_filled", "lgT_copied", "lg_filled", "lg_copied"))
        top_ready, tanh_ready, score_ready, onehot_ready = (sem(n) for n in ("top_ready", "tanh_ready", "score_ready", "onehot_ready"))
        rank_filled, slot_ready, xs_ready, scattered = (sem(n) for n in ("rank_filled", "slot_ready", "xs_ready", "scattered"))
        expert_ready = sem("expert_ready")
        sg_filled, su_filled, ssilu, sh_ready, sy_filled, sy_added = (sem(n) for n in ("sg_filled", "su_filled", "ssilu", "sh_ready", "sy_filled", "sy_added"))
        xg_loaded = sems("xg_loaded", LOADS)
        xgs_ready = sem("xgs_ready")
        gT_filled, gT_copied, gu_filled, rsilu, rh_ready = (sem(n) for n in ("gT_filled", "gT_copied", "gu_filled", "rsilu", "rh_ready"))
        hT_filled, hT_copied, ry_filled, ys_ready, ys_stored = (sem(n) for n in ("hT_filled", "hT_copied", "ry_filled", "ys_ready", "ys_stored"))
        gathered = sems("gathered", TILES)
        ffn_added, out_stored = sem("ffn_added"), sem("out_stored")
        waited = sem("waited")
        dve_step, pool_step = sem("dve_step"), sem("pool_step")
        uses = ["q0", "k0", "q1", "k1", "back", "oT", "wo", "xT", "qm0", "qm1"]
        lag = dict(q0=1, k0=1, q1=1, k1=1, back=-1, oT=-1, wo=-1, xT=3, qm0=1, qm1=1)
        filled = {n: sem("filled_" + n) for n in uses + ["qkv0", "qkv1"]}
        emptied = {n: sem("emptied_" + n) for n in uses + ["qkv0", "qkv1"]}
        a_stats, a_rstd, a_xn = sem("a_stats"), sem("a_rstd"), sem("a_xn")
        roped, rotated, part1, rem_ready, part2, part3, vx_ready = (sem(n) for n in ("roped", "rotated", "part1", "rem_ready", "part2", "part3", "vx_ready"))
        s_filled, s_reduced, m_split = sem("s_filled"), sem("s_reduced"), sem("m_split")
        st_filled, exp_done, pv_done, pv_copied = sem("st_filled"), sem("exp_done"), sem("pv_done"), sem("pv_copied")
        o_ready = sem("o_ready")

        def wait_apart(eng, s, value):
            eng.wait_ge(s, value)
            if not isinstance(value, int):
                eng.sem_inc(waited, 1)

        class Steps:

            def __init__(self, eng, s):
                self.eng, self.s, self.n, self.moved = eng, s, 0, 0

            def link(self, ins):
                ins.then_inc(self.s, 1)
                self.n += 1
                wait_apart(self.eng, self.s, self.n + self.moved)

            def loop(self, i, start, step, body, per, turns):
                first = self.n
                self.moved = (i - start) * (per // step)
                body()
                assert self.n == first + per, self.n - first
                self.n, self.moved = first + per * turns, 0

        PAR = 2
        FIRST_LOOPED, END_LOOPED = 2, B - 3 - (B - 3 - 2) % PAR

        class Turn:

            def __init__(self, i, u, looped):
                self.i, self.u, self.v, self.looped = i, u, 1 - u, looped
                has = lambda k: looped or 0 <= i + k < B
                self.e, self.m, self.pr, self.nx, self.f = (has(k) for k in (0, 1, 2, 3, -1))

            def from_(self, first):
                return self.looped or self.i >= first

        MADE = [0, 0, 0, 1, 3, 4, 6, 7, 9, 10, 12, 13, 15, 16, 16, 16]

        def attention(eng, turn, steps=None, per=0):
            for i in range(-3, FIRST_LOOPED):
                turn(Turn(i, i % PAR, False))
            with eng.Fori(FIRST_LOOPED // PAR, END_LOOPED // PAR) as w:
                i = w * PAR

                def body():
                    for k in range(PAR):
                        turn(Turn(i + k, k, True))
                if steps is None:
                    body()
                else:
                    steps.loop(i, FIRST_LOOPED, PAR, body, per, (END_LOOPED - FIRST_LOOPED) // PAR)
            for i in range(END_LOOPED, B + 1):
                turn(Turn(i, i % PAR, False))

        RLOOP = (3, SLOT_TILES - 4 - (SLOT_TILES - 7) % 2, 2)

        def routed(eng, turn, first):
            def run(j):
                turn(j, j % 2, lambda k: 0 <= j + k < SLOT_TILES and j + k >= 0)
            for j in range(first, RLOOP[0]):
                run(j)
            with eng.Fori(*RLOOP) as j:
                for k in range(RLOOP[2]):
                    turn(j + k, (RLOOP[0] + k) % 2, lambda _: True)
            for j in range(RLOOP[1], SLOT_TILES + 1):
                run(j)

        block = ctx.enter_context(nc.Block())

        @block.sync
        def _(sp):
            xv = x_in.rearrange("(c i p) d -> c p i d", p=P, i=CHUNK)
            sp.dma_start(x[:, 0:CHUNK, :], xv[0]).then_inc(x_loaded[0], 16)
            sp.dma_start(tab[:], tab_in).then_inc(tab_loaded, 16)
            sp.dma_start(tabb[:], tabb_in).then_inc(tab_loaded, 16)
            for c in range(1, CHUNKS):
                sp.dma_start(x[:, c * CHUNK:(c + 1) * CHUNK, :], xv[c]).then_inc(x_loaded[c], 16)
            sp.dma_start(wgate[:], wgate_in).then_inc(shw_loaded, 16)
            sp.dma_start(shgu[:], shgu_in).then_inc(shw_loaded, 16)
            sp.dma_start(shdn[:], shdn_in).then_inc(shw_loaded, 16)
            sp.wait_ge(zeros_set, 1)
            sp.dma_start(xs_dram.rearrange("(j p) d -> p j d", p=P), xg[:, 0:SLOT_TILES, :]).then_inc(zeros_stored, 16)
            sp.dma_start(rgu[:], rgu_in).then_inc(rw_loaded, 16)
            sp.dma_start(rdn[:], rdn_in).then_inc(rw_loaded, 16)
            sp.dma_start(wqkv[:], wqkv_in).then_inc(aw_loaded, 16)
            sp.dma_start(wo[:], wo_in).then_inc(aw_loaded, 16)
            for n in range(2):
                sp.wait_ge(scattered, 16 * TILES * (n + 1))
                for k in range(LOADS):
                    j0, j1 = k * LOAD, min((k + 1) * LOAD, SLOT_TILES)
                    sp.dma_start(xg[:, j0:j1, :], xs_dram[j0 * P:j1 * P, :].rearrange("(j p) d -> p j d", p=P)).then_inc(xg_loaded[k], 16)
                with sp.Fori(0, SLOT_TILES) as j:
                    sp.wait_ge(ys_ready, j + (n * SLOT_TILES + 1))
                    sp.dma_start(ys_dram[bass.ts(j, P), :], ys[:, bass.ds(j, 1), :].rearrange("p a d -> p (a d)")).then_inc(ys_stored, 16)
            ov = out.rearrange("(c i p) d -> c p i d", p=P, i=CHUNK)
            for c in range(CHUNKS):
                sp.wait_ge(ffn_added, TILES + (c + 1) * CHUNK)
                sp.dma_start(ov[c], x[:, c * CHUNK:(c + 1) * CHUNK, :]).then_inc(out_stored, 16)
            sp.wait_ge(out_stored, 16 * CHUNKS)

        @block.gpsimd
        def _(pool):
            g = nc.gpsimd
            st = Steps(pool, pool_step)
            g.memset(neghalf[:], -0.5).then_inc(consts_set, 1)
            pool.wait_ge(consts_set, 1)

            def ffn_rstd(n):
                for c in range(CHUNKS):
                    pool.wait_ge(ln_stats, n * CHUNKS + c + 1)
                    s = slice(c * CHUNK, (c + 1) * CHUNK)
                    st.link(g.tensor_scalar_add(rstd[:, s], meanvar[:, s, 1], EPS))
                    g.tensor_tensor(rstd[:, s], rstd[:, s], neghalf[:, s], ALU.pow).then_inc(ln_rstd, 1)
                    if n == 0 and c == 1:
                        g.memset(xg[:], 0.0).then_inc(zeros_set, 1)

            def scatter(n):
                pool.wait_ge(slot_ready, n + 1)
                if n == 0:
                    pool.wait_ge(zeros_stored, 16)
                for i in range(TILES):
                    pool.wait_ge(xs_ready, n * TILES + i + 1)
                    g.indirect_dma_start(
                        xs_dram, bass.IndirectOffsetOnAxis(ap=slot[:, i:i + 1], axis=0), xs[:, i, :], None,
                        bounds_check=SLOT_TILES * P - 1, oob_is_err=False).then_inc(scattered, 16)

            def stage(n):
                r = n * SLOT_TILES
                for k in range(LOADS):
                    pool.wait_ge(xg_loaded[k], 16 * (n + 1))

                def one(j, u):
                    if not isinstance(j, int) or j >= 2 or n:
                        wait_apart(pool, gT_filled, j + (r - 1))
                    g.tensor_copy(xgs[:, u, :], xg[:, bass.ds(j, 1), :].rearrange("p a d -> p (a d)")).then_inc(xgs_ready, 1)

                one(0, 0)
                one(1, 1)
                with pool.Fori(2, SLOT_TILES - SLOT_TILES % 2, 2) as j:
                    one(j, 0)
                    one(j + 1, 1)
                if SLOT_TILES % 2:
                    one(SLOT_TILES - 1, 0)

            def gather(n):
                pool.wait_ge(ys_stored, 16 * SLOT_TILES * (n + 1))
                for i in range(TILES):
                    g.indirect_dma_start(
                        yg[:, i, :], None, ys_dram, bass.IndirectOffsetOnAxis(ap=slot[:, i:i + 1], axis=0),
                        bounds_check=SLOT_TILES * P - 1, oob_is_err=False).then_inc(gathered[i], 16)

            ffn_rstd(0)
            for u in range(2):
                g.memset(kT[u][:].bitcast(F32), 0.0).then_inc(consts_set, 1)
                g.memset(vx[u][:], 0.0).then_inc(consts_set, 1)
                for t in range(2):
                    g.memset(parts[u][t][:].bitcast(F32), 0.0).then_inc(consts_set, 1)
            pool.wait_ge(consts_set, 9)
            for u in range(2):
                v5 = vx[u][:].rearrange("p t (f s g) c -> p (t f) s g c", f=2, s=2)
                for s_ in range(2):
                    g.memset(v5[:, :, s_, :, 16 + s_:17 + s_], 1.0).then_inc(consts_set, 1)
                for t in range(2):
                    g.memset(parts[u][t][:, 1, :, MCOL:MCOL + 3], 1.0).then_inc(consts_set, 1)
            scatter(0)
            stage(0)
            gather(0)

            def turn(T):
                i, u, v = T.i, T.u, T.v

                def split_max(t):
                    wait_apart(pool, s_reduced, 16 * (i + 1) + 8 * t + 8)
                    mc = [parts[v][t][:, 0, :, MCOL + k] for k in range(3)]
                    st.link(g.tensor_copy(mc[0], negmax[:, v, t, :]))
                    st.link(g.tensor_tensor(mrem[:, t, :], negmax[:, v, t, :], mc[0], ALU.subtract))
                    st.link(g.tensor_copy(mc[1], mrem[:, t, :]))
                    g.tensor_tensor(mc[2], mrem[:, t, :], mc[1], ALU.subtract).then_inc(m_split, 1)

                def rotate(t):
                    if T.from_(0):
                        wait_apart(pool, filled["qm1"], i + 1)
                    g.memset(parts[u][t][:, 0, :, MCOL:MCOL + 3], 0.0)
                    wait_apart(pool, roped, 2 * (i + 2) + t + 1)
                    g.tensor_tensor(rot[:, t, :], rc[:, t, :], rs[:, t, :], ALU.add).then_inc(rotated, 1)

                def remainder(t):
                    wait_apart(pool, part1, 2 * (i + 2) + t + 1)
                    r3 = lambda a: a[:, t, :].rearrange("p (q h d) -> p (q h) d", q=2, h=H)
                    flat = parts[u][t][:].rearrange("p q h c -> p (q h) c")
                    g.tensor_tensor(r3(rem), r3(rot), flat[:, :, 2 * DH:3 * DH], ALU.subtract).then_inc(rem_ready, 1)

                def third(t):
                    wait_apart(pool, part2, 2 * (i + 2) + t + 1)
                    for q, at in ((0, 3), (1, 0)):
                        ins = g.tensor_tensor(
                            parts[u][t][:, q, :, at * DH:(at + 1) * DH], rem[:, t, q * D:(q + 1) * D].rearrange("p (h d) -> p h d", h=H),
                            parts[u][t][:, q, :, 5 * DH:6 * DH], ALU.subtract)
                    ins.then_inc(part3, 1)

                def values(t):
                    vs = vstage[:, v, t, :].rearrange("p (f s g d) -> p f s g d", f=2, s=2, g=4)
                    vd = vx[v][:, t].rearrange("p (f s g) c -> p f s g c", f=2, s=2)
                    for k in range(2):
                        ins = g.tensor_copy(vd[:, :, k, :, k * DH:(k + 1) * DH], vs[:, :, k])
                    if t == 1:
                        ins.then_inc(vx_ready, 1)

                if T.pr:
                    rotate(0)
                    rotate(1)
                if T.m:
                    wait_apart(pool, emptied["qkv1"], i + 2)
                    if T.from_(1):
                        wait_apart(pool, pv_done, 4 * i)
                    values(0)
                    values(1)
                if T.pr:
                    remainder(0)
                    remainder(1)
                if T.nx:
                    wait_apart(pool, a_stats, i + 4)
                    st.link(g.tensor_scalar_add(rstd2[:, v, :], meanvar2[:, v, :, 1], EPS))
                    g.tensor_tensor(rstd2[:, v, :], rstd2[:, v, :], neghalf[:, 0:2], ALU.pow).then_inc(a_rstd, 1)
                if T.pr:
                    third(0)
                if T.m:
                    split_max(0)
                if T.pr:
                    third(1)
                if T.m:
                    split_max(1)

            attention(pool, turn, st, 2 * (1 + 6))
            ffn_rstd(1)
            scatter(1)
            stage(1)
            gather(1)

        @block.scalar
        def _(act):
            a = nc.scalar

            def ffn(n):
                for c in range(CHUNKS):
                    act.wait_ge(xT_filled, n * CHUNKS + c + 1)
                    a.copy(xnT[:, c * 512:(c + 1) * 512], bank[c % 2][:]).then_inc(xT_copied, 1)

                def silu(c):
                    act.wait_ge(sg_filled, n * CHUNKS + c + 1)
                    if n * CHUNKS + c:
                        act.wait_ge(sh_ready, n * CHUNKS + c)
                    for k in range(2):
                        ins = a.activation(sgate[:, k, :], bank[2 + k][:], ACT.Silu)
                        ins.then_inc(ssilu, 1)

                silu(0)
                act.wait_ge(top_ready, n + 1)
                a.activation(tanh_half[:], top[:], ACT.Tanh, scale=0.5).then_inc(tanh_ready, 1)
                act.wait_ge(score_ready, n + 1)
                for i in range(TILES):
                    a.activation(xs[:, i, :], xn[:, i, :], ACT.Copy, scale=score[:, i:i + 1]).then_inc(xs_ready, 1)
                for c in range(1, CHUNKS):
                    silu(c)

                r = n * SLOT_TILES

                def copy_gT(j, u):
                    act.wait_ge(gT_filled, j + (r + 1))
                    a.copy(xgT[:, u, :], bank[u][:, 0:P]).then_inc(gT_copied, 1)

                def turn(j, u, has):
                    if has(1):
                        act.wait_ge(gu_filled, j + (r + 2))
                        if not isinstance(j, int) or j >= 1:
                            act.wait_ge(rh_ready, j + r)
                        a.activation(rsg[:, 1 - u, :], bank[3 - u][:, 0:F], ACT.Silu).then_inc(rsilu, 1)
                    if has(3):
                        copy_gT(j + 3, 1 - u)
                    if has(0):
                        act.wait_ge(hT_filled, j + (r + 1))
                        if not isinstance(j, int) or j >= 2 or n:
                            act.wait_ge(ry_filled, j + (r - 1))
                        a.copy(rhT[:, u, :, :].rearrange("p k s -> p (k s)"), bank[4 + u][:, 0:2 * P]).then_inc(hT_copied, 1)

                copy_gT(0, 0)
                copy_gT(1, 1)
                routed(act, turn, -1)

            def turn(T):
                i, u, v = T.i, T.u, T.v

                def exponentials(h):
                    act.wait_ge(st_filled, 16 * i + h + 1)
                    if T.from_(2) or (T.i == 1) or h >= 8:
                        act.wait_ge(pv_done, 4 * i + (h // 4 - 1))
                    a.activation(probs[:, h % 8, :], stbank[h % 2][:], ACT.Exp, scale=float(DH) ** -0.5).then_inc(exp_done, 1)

                def copy_keys(t):
                    name = f"k{t}"
                    act.wait_ge(filled[name], i + 2)
                    src = work[uses.index(name) % 2][:].bitcast(BF16).rearrange("p (r s) -> p r s", r=8)
                    for k in range(2):
                        ins = a.copy(kT[v][64 * k:64 * k + 64, :, k, t * P:(t + 1) * P], src[64 * k:64 * k + 64])
                    ins.then_inc(emptied[name], 1)

                def part(t, rows, src, into, ready, done):
                    act.wait_ge(ready, 2 * (i + 2) + t + 1)
                    if ready is rotated and T.from_(0):
                        act.wait_ge(filled["qm1"], i + 1)
                    for q in range(2):
                        part_of = src[:, t, q * D:(q + 1) * D].rearrange("p (h d) -> p h d", h=H)
                        dst = parts[u][t][:, q, :, 0:MCOL].rearrange("p h (s d) -> p h s d", s=6)[:, :, into[q], :]
                        ins = a.copy(dst, part_of.unsqueeze(2).to_broadcast([P, H, rows, DH]))
                    ins.then_inc(done, 1)

                first = lambda t: part(t, 3, rot, (slice(0, 6, 2), slice(1, 4)), rotated, part1)
                second = lambda t: part(t, 2, rem, (slice(1, 6, 4), slice(4, 6)), rem_ready, part2)
                for s_ in range(16):
                    if T.m and s_ < 2:
                        copy_keys(s_)
                    if T.e:
                        exponentials(s_)
                    if s_ == 2 and T.f:
                        act.wait_ge(pv_done, 4 * i)
                        a.copy(pvs[:].rearrange("p f s -> p (f s)"), pvbank[v][:]).then_inc(pv_copied, 1)
                    if s_ == 6 and T.f:
                        act.wait_ge(filled["oT"], i)
                        a.copy(oT[:], work[1][:, 0:L]).then_inc(emptied["oT"], 1)
                    if s_ == 11 and T.nx:
                        act.wait_ge(filled["xT"], i + 4)
                        a.copy(xnT2[:, v, :], work[1][:, 0:L]).then_inc(emptied["xT"], 1)
                    if T.pr:
                        if s_ in (4, 5):
                            first(s_ - 4)
                        if s_ in (7, 9):
                            second((s_ - 7) // 2)

            ffn(0)
            attention(act, turn)
            ffn(1)

        @block.vector
        def _(dve):
            v_ = nc.vector
            st = Steps(dve, dve_step)

            def normalise(o_, x_, mv, r_):
                return v_.tensor_scalar(o_, x_, mv, r_, ALU.subtract, ALU.mult)

            def ffn(n):
                def ln(c):
                    dve.wait_ge(ln_rstd, n * CHUNKS + c + 1)
                    for i in range(c * CHUNK, (c + 1) * CHUNK):
                        ins = normalise(xn[:, i, :], x[:, i, :], meanvar[:, i, 0:1], rstd[:, i:i + 1])
                        ins.then_inc(xn_ready, 1)

                for c in range(CHUNKS):
                    if n == 0:
                        dve.wait_ge(x_loaded[c], 16)
                    else:
                        dve.wait_ge(emptied["wo"], 2 * c + 2)
                    for i in range(c * CHUNK, (c + 1) * CHUNK):
                        ins = v_.bn_stats(stats[:, i, :], x[:, i, :])
                    st.link(ins)
                    for i in range(c * CHUNK, (c + 1) * CHUNK):
                        ins = v_.bn_aggr(meanvar[:, i, :], stats[:, i, :])
                    ins.then_inc(ln_stats, 1)
                    if c:
                        ln(c - 1)
                ln(CHUNKS - 1)

                dve.wait_ge(lgT_filled, n + 1)
                v_.tensor_copy(lgT[:], bank[7][:]).then_inc(lgT_copied, 1)
                dve.wait_ge(lg_filled, n + 1)
                src = bank[0][:].rearrange("p (c g k) -> p g c k", c=4, g=4)[:, :, :, 0:E]
                st.link(v_.tensor_copy(lg[:].rearrange("p (g c) e -> p g c e", g=4), src))
                lg_all = lambda a_: a_[:].unsqueeze(2).to_broadcast([P, TILES, E])
                v_.tensor_reduce(top[:], lg[:], AX.X, ALU.max).then_inc(top_ready, 1)
                dve.wait_ge(top_ready, n + 1)
                st.link(v_.tensor_tensor(is_top[:], lg[:], lg_all(top), ALU.is_equal))
                em8 = eminus8.unsqueeze(1).to_broadcast([P, TILES, E])
                st.link(v_.tensor_tensor(is_top[:], is_top[:], em8, ALU.mult))
                st.link(v_.tensor_reduce(first_top[:], is_top[:], AX.X, ALU.min))
                st.link(v_.tensor_tensor(onehot[:], em8, lg_all(first_top), ALU.is_equal))
                v_.tensor_copy(onehotb[:], onehot[:]).then_inc(onehot_ready, 1)
                dve.wait_ge(tanh_ready, n + 1)
                v_.tensor_scalar(score[:], tanh_half[:], 0.5, 0.5, ALU.mult, ALU.add).then_inc(score_ready, 1)

                def shared_hidden(c):
                    k0 = n * CHUNKS + c
                    dve.wait_ge(ssilu, 2 * k0 + 2)
                    dve.wait_ge(su_filled, k0 + 1)
                    if k0 >= 2:
                        dve.wait_ge(sy_filled, k0 - 1)
                    st.link(v_.tensor_tensor(sh[:, c % 2, 0, :], sgate[:, 0, :], bank[4][:], ALU.mult))
                    v_.tensor_tensor(sh[:, c % 2, 1, :], sgate[:, 1, :], bank[5][:], ALU.mult).then_inc(sh_ready, 1)

                def shared_add(c):
                    dve.wait_ge(sy_filled, n * CHUNKS + c + 1)
                    s = slice(c * CHUNK, (c + 1) * CHUNK)
                    xc = x[:, s, :].rearrange("p i d -> p (i d)")
                    v_.scalar_tensor_tensor(out=xc, in0=bank[6][:], scalar=0.5, in1=xc, op0=ALU.mult, op1=ALU.add).then_inc(sy_added, 1)

                dve.wait_ge(rank_filled, n + 1)
                rank = bank[7][:, 0:(TILES + 1) * E].rearrange("p (i e) -> p i e", e=E)
                st.link(v_.tensor_copy(total[:], rank[:, TILES, :]))
                st.link(v_.tensor_tensor(over[:], total[:].unsqueeze(2).to_broadcast([P, E, 16]),
                                         steps128.unsqueeze(1).to_broadcast([P, E, 16]), ALU.is_gt))
                st.link(v_.tensor_reduce(etiles[:], over[:], AX.X, ALU.add))
                st.link(v_.tensor_tensor(etb[:], before, etiles[:].unsqueeze(1).to_broadcast([P, E, E]), ALU.mult))
                st.link(v_.tensor_reduce(estart[:], etb[:], AX.X, ALU.add))
                st.link(v_.tensor_scalar(estart128[:], estart[:], float(P), None, ALU.mult))
                st.link(v_.tensor_tensor(slot8[:], rank[:, 0:TILES, :], estart128[:].unsqueeze(1).to_broadcast([P, TILES, E]), ALU.add))
                st.link(v_.tensor_tensor(slot8[:], slot8[:], onehot[:], ALU.mult))
                st.link(v_.tensor_reduce(slotf[:], slot8[:], AX.X, ALU.add))
                v_.tensor_copy(slot[:], slotf[:]).then_inc(slot_ready, 1)
                st.link(v_.tensor_tensor(eend[:], estart[:], etiles[:], ALU.add))
                st.link(v_.tensor_tensor(ended[:], eend[0:1, :].unsqueeze(1).to_broadcast([1, SLOT_TILES, E]),
                                         tile_no[0:1, :].unsqueeze(2).to_broadcast([1, SLOT_TILES, E]), ALU.is_le))
                st.link(v_.tensor_reduce(expertf[:], ended[:], AX.X, ALU.add))
                st.link(v_.tensor_scalar(expertf[:], expertf[:], float(E - 1), None, ALU.min))
                v_.tensor_copy(expert[:], expertf[:]).then_inc(expert_ready, 1)

                shared_hidden(0)
                for c in range(1, CHUNKS):
                    shared_hidden(c)
                    shared_add(c - 1)
                shared_add(CHUNKS - 1)

                r = n * SLOT_TILES

                def turn(j, u, has):
                    if has(1):
                        dve.wait_ge(rsilu, j + (r + 2))
                        if not isinstance(j, int) or j >= 1 or n:
                            dve.wait_ge(hT_filled, j + r)
                        v_.tensor_tensor(rh[:, 1 - u, :], rsg[:, 1 - u, :], bank[3 - u][:, F:2 * F], ALU.mult).then_inc(rh_ready, 1)
                    if has(-1):
                        dve.wait_ge(ry_filled, j + r)
                        v_.tensor_copy(ys[:, bass.ds(j - 1, 1), :].rearrange("p a d -> p (a d)"), bank[6 + (1 - u)][:, 0:D]).then_inc(ys_ready, 1)

                routed(dve, turn, -1)
                if n:
                    add_experts(n, 0, TILES)

            def add_experts(n, i0, i1):
                if i0 == 0:
                    dve.wait_ge(sy_added, CHUNKS * (n + 1))
                for i in range(i0, i1):
                    dve.wait_ge(gathered[i], 16 * (n + 1))
                    v_.scalar_tensor_tensor(out=x[:, i, :], in0=yg[:, i, :], scalar=0.5, in1=x[:, i, :], op0=ALU.mult, op1=ALU.add).then_inc(ffn_added, 1)

            def turn(T):
                i, u, v = T.i, T.u, T.v

                def q_copy(name, t):
                    dve.wait_ge(filled[name], i + 2)
                    v_.tensor_copy(qT[v][:, :, t * P:(t + 1) * P],
                                   work[uses.index(name) % 2][:].bitcast(BF16).rearrange("p (r s) -> p r s", r=8)).then_inc(emptied[name], 1)

                def maxima(k):
                    dve.wait_ge(s_filled, 16 * (i + 1) + k + 1)
                    t, pair = k // 8, k % 8
                    v_.tensor_reduce(negmax[:, v, t, 2 * pair:2 * pair + 2], sbank[k % 2][:].rearrange("p (a s) -> p a s", a=2),
                                     AX.X, ALU.max, negate=True).then_inc(s_reduced, 1)

                def rope(t):
                    name = f"qkv{t}"
                    dve.wait_ge(filled[name], i + 3)
                    if T.from_(-1):
                        dve.wait_ge(rotated, 2 * (i + 1) + t + 1)
                    qk = sbank[t][:, 0:2 * D]
                    pairs, turned, sn = (a_.rearrange("p (r two) -> p r two", two=2) for a_ in (qk, rs[:, t, :], sin[:, t, :]))
                    v_.tensor_tensor(rc[:, t, :], qk, cos[:, t, :], ALU.mult)
                    v_.tensor_tensor(turned[:, :, 0], pairs[:, :, 1], sn[:, :, 0], ALU.mult)
                    v_.tensor_tensor(turned[:, :, 1], pairs[:, :, 0], sn[:, :, 1], ALU.mult).then_inc(roped, 1)
                    if T.from_(0):
                        dve.wait_ge(vx_ready, i + 1)
                    v_.tensor_copy(vstage[:, u, t, :], sbank[t][:, 2 * D:3 * D]).then_inc(emptied[name], 1)

                def tile(t, w=1):
                    return x[:, bass.ds(t, w), :].rearrange("p a d -> p (a d)")

                if not T.looped and i < 0:
                    add_experts(0, *((0, 4), (4, 10), (10, 16))[i + 3])
                for s_ in range(16):
                    if s_ < 2:
                        if T.pr:
                            rope(s_)
                        if T.m:
                            q_copy(f"q{s_}", s_)
                    if T.m:
                        for k in range(MADE[s_ - 1] if s_ else 0, MADE[s_]):
                            maxima(k)
                    if s_ == 3 and T.f:
                        dve.wait_ge(filled["back"], i)
                        st.link(v_.reciprocal(rden[:], work[0][:].rearrange("p (x c) -> p x c", x=16)[:, :, 16:18]))
                        bk = work[0][:].rearrange("p (x g c) -> p x g c", x=4, g=4)
                        ov = oatt[:].rearrange("p t (f s g d) -> p (t f) s g d", f=2, s=2, g=4)
                        rv = rden[:].rearrange("p (x g) s -> p x g s", x=4)
                        for s2 in range(2):
                            ins = v_.tensor_tensor(ov[:, :, s2], bk[:, :, :, s2 * DH:(s2 + 1) * DH],
                                                   rv[:, :, :, s2].unsqueeze(3).to_broadcast([P, 4, 4, DH]), ALU.mult)
                        ins.then_inc(emptied["back"], 1)
                    if s_ == 6 and T.nx:
                        dve.wait_ge(ffn_added, 2 * (i + 3) + 2)
                        for t in range(2):
                            ins = v_.bn_stats(stats2[:, t, :], tile(2 * (i + 3) + t))
                        st.link(ins)
                        for t in range(2):
                            ins = v_.bn_aggr(meanvar2[:, v, t, :], stats2[:, t, :])
                        ins.then_inc(a_stats, 1)
                    if s_ == 9 and T.nx:
                        dve.wait_ge(a_rstd, i + 4)
                        for t in range(2):
                            ins = normalise(xn2[:, v, t, :], tile(2 * (i + 3) + t), meanvar2[:, v, t, 0:1], rstd2[:, v, t:t + 1])
                            ins.then_inc(a_xn, 1)
                    if s_ == 8 and T.f:
                        dve.wait_ge(filled["wo"], i)
                        v_.tensor_tensor(tile(2 * (i - 1), 2), work[0][:, 0:L], tile(2 * (i - 1), 2), ALU.add).then_inc(emptied["wo"], 1)
                    if s_ == 11 and T.m:
                        q_copy("qm0", 0)
                if T.m:
                    q_copy("qm1", 1)

            ffn(0)
            attention(dve, turn, st, 2 * 2)
            ffn(1)

        @block.tensor
        def _(pe):
            t_ = nc.tensor

            def mm(o_, l, r, start=True, stop=True, **k):
                return t_.matmul(o_, l, r, start=start, stop=stop, **k)

            def ffn(n):
                if n == 0:
                    pe.wait_ge(tab_loaded, 32)
                else:
                    pe.wait_ge(emptied["wo"], B)
                    pe.wait_ge(exp_done, 16 * B)
                for c in range(CHUNKS):
                    pe.wait_ge(xn_ready, (n * CHUNKS + c + 1) * CHUNK)
                    if c >= 2:
                        pe.wait_ge(xT_copied, n * CHUNKS + c - 1)
                    for i in range(CHUNK):
                        ins = t_.transpose(bank[c % 2][:, i * P:(i + 1) * P], xn[:, c * CHUNK + i, :], ident)
                    ins.then_inc(xT_filled, 1)
                if n == 0:
                    pe.wait_ge(shw_loaded, 48)
                for c in range(CHUNKS):
                    pe.wait_ge(xT_copied, n * CHUNKS + c + 1)
                    ins = mm(bank[7][32 * c:32 * c + 32, :], wgate[:], xnT[:, c * 512:(c + 1) * 512])
                ins.then_inc(lgT_filled, 1)

                def shared_gate(c):
                    k0 = n * CHUNKS + c
                    if k0:
                        pe.wait_ge(ssilu, 2 * k0)
                    for k in range(2):
                        ins = mm(bank[2 + k][:], shgu[:, k * P:(k + 1) * P], xnT[:, c * 512:(c + 1) * 512])
                    ins.then_inc(sg_filled, 1)

                def shared_up(c):
                    k0 = n * CHUNKS + c
                    if k0:
                        pe.wait_ge(sh_ready, k0)
                    for k in range(2):
                        ins = mm(bank[4 + k][:], shgu[:, F + k * P:F + (k + 1) * P], xnT[:, c * 512:(c + 1) * 512])
                    ins.then_inc(su_filled, 1)

                def shared_down(c):
                    k0 = n * CHUNKS + c
                    pe.wait_ge(sh_ready, k0 + 1)
                    if k0:
                        pe.wait_ge(sy_added, k0)
                    for i in range(CHUNK):
                        for k in range(2):
                            ins = mm(bank[6][:, i * P:(i + 1) * P], sh[:, c % 2, k, i * P:(i + 1) * P], shdn[:, k, :],
                                     start=(k == 0), stop=(k == 1))
                    ins.then_inc(sy_filled, 1)

                shared_gate(0)
                pe.wait_ge(lgT_copied, n + 1)
                for c in range(4):
                    ins = t_.transpose(bank[0][:, c * P:(c + 1) * P], lgT[:, c * P:(c + 1) * P], ident)
                ins.then_inc(lg_filled, 1)
                shared_up(0)
                pe.wait_ge(onehot_ready, n + 1)
                rank = bank[7][:, 0:(TILES + 1) * E]
                oh = onehotb[:]
                mm(rank[:, 0:TILES * E], upper, oh.rearrange("p i e -> p (i e)"), stop=False, skip_group_check=True)
                for i in range(TILES):
                    w = TILES - i
                    ins = mm(rank[:, (i + 1) * E:].rearrange("p (i e) -> p i e", e=E), onesb,
                             oh[:, i:i + 1, :].to_broadcast([P, w, E]), start=False, stop=(i == TILES - 1), skip_group_check=True)
                ins.then_inc(rank_filled, 1)
                for c in range(1, CHUNKS):
                    shared_gate(c)
                    shared_down(c - 1)
                    shared_up(c)
                shared_down(CHUNKS - 1)

                r = n * SLOT_TILES
                if n == 0:
                    pe.wait_ge(rw_loaded, 32)
                pe.wait_ge(expert_ready, n + 1)

                def turn_g(j, u):
                    pe.wait_ge(xgs_ready, j + (r + 1))
                    if not isinstance(j, int) or j >= 2:
                        pe.wait_ge(gT_copied, j + (r - 1))
                    t_.transpose(bank[u][:, 0:P], xgs[:, u, :], ident).then_inc(gT_filled, 1)

                def turn(j, u, has):
                    if has(1):
                        ex = t_.value_load(expert[0:1, bass.ds(j + 1, 1)], min_val=0, max_val=E - 1)
                        pe.wait_ge(gT_copied, j + (r + 2))
                        if not isinstance(j, int) or j >= 1 or n:
                            pe.wait_ge(rh_ready, j + r)
                        mm(bank[3 - u][:], xgT[:, 1 - u, :], rgu[:, bass.ds(ex * (2 * F), 2 * F)]).then_inc(gu_filled, 1)
                    if has(3):
                        turn_g(j + 3, 1 - u)
                    if has(0):
                        pe.wait_ge(rh_ready, j + (r + 1))
                        for k in range(2):
                            ins = t_.transpose(bank[4 + u][:, k * P:(k + 1) * P], rh[:, u, k * P:(k + 1) * P], ident)
                        ins.then_inc(hT_filled, 1)
                    if has(-1):
                        v = 1 - u
                        ex = t_.value_load(expert[0:1, bass.ds(j - 1, 1)], min_val=0, max_val=E - 1)
                        pe.wait_ge(hT_copied, j + r)
                        if not isinstance(j, int) or j >= 3:
                            pe.wait_ge(ys_ready, j + (r - 2))
                        for k in range(2):
                            ins = mm(bank[6 + v][:, 0:D], rhT[:, v, k, :], rdn[:, bass.ds(ex * (2 * D) + k * D, D)], start=(k == 0), stop=(k == 1))
                        ins.then_inc(ry_filled, 1)

                turn_g(0, 0)
                turn_g(1, 1)
                routed(pe, turn, -1)

            def turn(T):
                i, u, v = T.i, T.u, T.v

                def work_bank(name):
                    at = uses.index(name)
                    for back in range(2, 3 * len(uses), 2):
                        before_ = uses[(at - back) % len(uses)]
                        seq = i - (back - at + len(uses) - 1) // len(uses) + lag[before_]
                        if T.looped or 0 <= seq < B:
                            pe.wait_ge(emptied[before_], seq + 1)
                            break
                    return work[at % 2]

                def parts_turned(name, t, q):
                    w = work_bank(name)[:].bitcast(BF16)
                    for k in range(H // 2):
                        ins = t_.transpose(w[:, k * P:(k + 1) * P],
                                           parts[v][t][:, q, 2 * k:2 * k + 2, :].rearrange("p a c -> p (a c)"), identb)
                    ins.then_inc(filled[name], 1)

                def scores(k):
                    t, pair = k // 8, k % 8
                    if k == 0:
                        for name in ("q0", "k0", "k1"):
                            pe.wait_ge(emptied[name], i + 2)
                    if k == 8:
                        pe.wait_ge(emptied["q1"], i + 2)
                    if k < 2 and T.pr:
                        pe.wait_ge(emptied[f"qkv{k}"], i + 3)
                    elif T.from_(0) or k >= 2:
                        pe.wait_ge(s_reduced, 16 * (i + 1) + (k - 1))
                    mm(sbank[k % 2][:], qT[v][:, pair, t * P:(t + 1) * P],
                       kT[v][:, pair, :, :].rearrange("p a s -> p (a s)")).then_inc(s_filled, 1)

                def scores_t(h):
                    if h == 0:
                        for name in ("qm0", "qm1"):
                            pe.wait_ge(emptied[name], i + 1)
                    if T.from_(1) or h >= 2:
                        pe.wait_ge(exp_done, 16 * i + (h - 1))
                    for k in range(2):
                        ins = mm(stbank[h % 2][:, k * L:(k + 1) * L], kT[u][:, h // 2, h % 2, k * P:(k + 1) * P], qT[u][:, h // 2, :])
                    ins.then_inc(st_filled, 1)

                def values(k):
                    if k == 0:
                        pe.wait_ge(vx_ready, i + 1)
                        if T.from_(2):
                            pe.wait_ge(pv_copied, i - 1)
                    pe.wait_ge(exp_done, 16 * i + 4 * k + 4)
                    half, sub = k // 2, k % 2
                    for c in range(2):
                        for g in range(4):
                            h = 4 * k + g
                            first = sub == 0 and c == 0
                            ins = mm(pvbank[u][32 * g:32 * g + 32, half * L:(half + 1) * L], vx[u][:, c, h, :],
                                     probs[:, h % 8, c * L:(c + 1) * L], start=first, stop=(sub == 1 and c == 1))
                    ins.then_inc(pv_done, 1)

                def project(t):
                    if t == 0:
                        pe.wait_ge(emptied["xT"], i + 3)
                    if T.from_(0):
                        pe.wait_ge(s_reduced, 16 * (i + 1))
                    mm(sbank[t][:, 0:3 * D], xnT2[:, u, t * P:(t + 1) * P], wqkv[:]).then_inc(filled[f"qkv{t}"], 1)

                if T.pr:
                    project(0)
                    project(1)
                for s_ in range(16):
                    if T.m and s_ < 2:
                        if s_ == 0:
                            pe.wait_ge(part3, 2 * (i + 1) + 2)
                        parts_turned(f"q{s_}", s_, 0)
                        parts_turned(f"k{s_}", s_, 1)
                    if T.e:
                        scores_t(s_)
                    if T.e and s_ in (5, 9, 13):
                        values(s_ // 4 - 1)
                    if s_ == 3 and T.f:
                        w = work_bank("back")
                        pe.wait_ge(pv_copied, i)
                        for c in range(4):
                            ins = t_.transpose(w[:, c * P:(c + 1) * P], pvs[:, c % 2, (c // 2) * P:(c // 2 + 1) * P], ident)
                        ins.then_inc(filled["back"], 1)
                    if T.m:
                        for k in range(MADE[s_ - 1] if s_ else 0, MADE[s_]):
                            scores(k)
                    if s_ == 6 and T.f:
                        w = work_bank("oT")
                        pe.wait_ge(emptied["back"], i)
                        for t in range(2):
                            ins = t_.transpose(w[:, t * P:(t + 1) * P], oatt[:, t, :], ident)
                        ins.then_inc(filled["oT"], 1)
                    if s_ == 8 and T.f:
                        w = work_bank("wo")
                        pe.wait_ge(emptied["oT"], i)
                        for t in range(2):
                            ins = mm(w[:, t * P:(t + 1) * P], oT[:, t * P:(t + 1) * P], wo[:])
                        ins.then_inc(filled["wo"], 1)
                    if s_ == 11 and T.nx:
                        w = work_bank("xT")
                        pe.wait_ge(a_xn, 2 * (i + 3) + 2)
                        for t in range(2):
                            ins = t_.transpose(w[:, t * P:(t + 1) * P], xn2[:, v, t, :], ident)
                        ins.then_inc(filled["xT"], 1)
                    if s_ == 11 and T.m:
                        pe.wait_ge(m_split, 2 * (i + 1) + 1)
                        parts_turned("qm0", 0, 0)
                if T.m:
                    pe.wait_ge(m_split, 2 * (i + 1) + 2)
                    parts_turned("qm1", 1, 0)
                if T.e:
                    values(3)

            ffn(0)
            pe.wait_ge(aw_loaded, 32)
            for s_ in (gT_copied, rh_ready, hT_copied, ys_ready):
                pe.wait_ge(s_, SLOT_TILES)
            attention(pe, turn)
            ffn(1)


TAB_COLS = P + 1024 + 88 + SLOT_TILES
TABB_COLS = 3 * P


def tables():
    f = np.float32
    freqs = np.exp((-np.log(10000.0)).astype(f) * np.arange(0, DH, 2, dtype=f) / f(DH)).astype(f)
    angle = (np.arange(L, dtype=f)[:, None] * freqs).astype(f)
    cos = np.tile(np.repeat(np.cos(angle), 2, axis=1), (1, 2 * H)).reshape(2, P, 2 * D).transpose(1, 0, 2).reshape(P, 4 * D)
    signed = np.stack([-np.sin(angle), np.sin(angle)], axis=-1).reshape(L, DH)
    sin = np.tile(signed, (1, 2 * H)).reshape(2, P, 2 * D).transpose(1, 0, 2).reshape(P, 4 * D)
    row = lambda a: np.tile(np.asarray(a, f).reshape(1, -1), (P, 1))
    tab = np.concatenate([np.eye(P, dtype=f), cos, sin, row(np.arange(16) * P), row(np.tril(np.ones((E, E)), -1)),
                          row(np.arange(E) - E), row(np.arange(SLOT_TILES))], axis=1)
    tabb = np.concatenate([np.eye(P), np.triu(np.ones((P, P)), 1), np.ones((P, P))], axis=1)
    return np.ascontiguousarray(tab, f), tabb


def kernel(L0_attn_x, L0_attn_W_q, L0_attn_W_k, L0_attn_W_v, L0_attn_W_o, L0_ffn_gate_w, L0_ffn_shared_gate,
           L0_ffn_shared_up, L0_ffn_shared_down, L0_ffn_r_gate, L0_ffn_r_up, L0_ffn_r_down):
    import ml_dtypes
    import concourse.bacc as bacc
    from concourse.bass_utils import run_bass_kernel_spmd as run

    tab, tabb = tables()
    gate = np.zeros((D, 32), np.float32)
    gate[:, 0:E] = np.transpose(L0_ffn_gate_w)
    cols = lambda *a: np.concatenate([np.transpose(w) for w in a], axis=1)
    two = np.concatenate([np.transpose(L0_ffn_r_gate, (2, 0, 1)), np.transpose(L0_ffn_r_up, (2, 0, 1))], axis=2)
    arrays = {
        "x": np.reshape(L0_attn_x, (N, D)),
        "wqkv": cols(L0_attn_W_q, L0_attn_W_k, L0_attn_W_v),
        "wo": np.transpose(L0_attn_W_o),
        "wgate": gate,
        "shgu": cols(L0_ffn_shared_gate, L0_ffn_shared_up),
        "shdn": np.transpose(np.reshape(np.transpose(L0_ffn_shared_down), (2, P, D)), (1, 0, 2)),
        "rgu": np.reshape(two, (D, E * 2 * F)),
        "rdn": np.reshape(np.transpose(np.reshape(L0_ffn_r_down, (E, D, 2, P)), (3, 0, 2, 1)), (P, E * 2 * D)),
        "tab": tab,
        "tabb": tabb.astype(ml_dtypes.bfloat16),
    }
    arrays = {k: np.ascontiguousarray(v) for k, v in arrays.items()}
    nc = bacc.Bacc("TRN2", target_bir_lowering=False, num_devices=1)
    aps = [nc.dram_tensor("in_" + k, v.shape, mybir.dt.from_np(v.dtype), kind="ExternalInput").ap() for k, v in arrays.items()]
    out = nc.dram_tensor("out_x", (N, D), F32, kind="ExternalOutput").ap()
    build(nc, *aps, out)
    r = run(nc, [{"in_" + k: v for k, v in arrays.items()}], core_ids=[0])
    return np.reshape(r.results[0]["out_x"], (B, L, D))
```

```python
from contextlib import ExitStack

import concourse.bass as bass
from concourse import mybir
from concourse.alu_op_type import AluOpType as ALU
import numpy as np

ACT = mybir.ActivationFunctionType
AX = mybir.AxisListType
F32 = mybir.dt.float32
BF16 = mybir.dt.bfloat16
I32 = mybir.dt.int32
U32 = mybir.dt.uint32

P = 128
D = 128
B, L = 8, 256
H, DH = 16, 8
F = 256
E = 8
N = B * L
TILES = N // P
CHUNK = 4
CHUNKS = TILES // CHUNK
SLOT_TILES = TILES + E - 1
LOAD = 4
LOADS = -(-SLOT_TILES // LOAD)
ROW = D + 1
EPS = 1e-5
KROWS = 64
MCOL = 6 * DH


def build(nc, x_in, wqkv_in, wo_in, wgate_in, shgu_in, shdn_in, rgu_in, rdn_in, tab_in, tabb_in, out):
    ctx = ExitStack()
    with ctx:
        def sb(name, shape, dt):
            return ctx.enter_context(nc.sbuf_tensor(name, shape, dt))

        def sem(name):
            return ctx.enter_context(nc.semaphore(name))

        def sems(name, n):
            return [sem(f"{name}{i}") for i in range(n)]

        x = sb("x", [P, TILES, D], F32)
        wqkv = sb("wqkv", [D, 3 * D], F32)
        wo = sb("wo", [D, D], F32)
        wgate = sb("wgate", [D, 32], F32)
        shgu = sb("shgu", [D, 2 * F], F32)
        shdn = sb("shdn", [P, 2, D], F32)
        rgu = sb("rgu", [D, E * 2 * F], F32)
        rdn = sb("rdn", [P, E * 2 * D], F32)
        tab = sb("tab", [P, TAB_COLS], F32)
        tabb = sb("tabb", [P, TABB_COLS], BF16)
        ident = tab[:, 0:P]
        cos = tab[:, P:P + 2 * DH].rearrange("p (t n) -> p t n", t=2)
        sin = tab[:, P + 2 * DH:P + 4 * DH].rearrange("p (t n) -> p t n", t=2)
        o = P + 4 * DH
        steps128 = tab[:, o:o + 16]
        before = tab[:, o + 16:o + 80].rearrange("p (e f) -> p e f", e=E)
        eminus8 = tab[:, o + 80:o + 88]
        tile_no = tab[:, o + 88:o + 88 + SLOT_TILES]
        token_no = tab[:, o + 88 + SLOT_TILES:o + 88 + SLOT_TILES + TILES]
        spare_no = tab[:, o + 88 + SLOT_TILES + TILES:TAB_COLS]
        identb = tabb[:, 0:P]
        upper = tabb[:, P:2 * P]
        onesb = tabb[:, 2 * P:3 * P]

        stats = sb("stats", [P, TILES, 6], F32)
        meanvar = sb("meanvar", [P, TILES, 2], F32)
        rstd = sb("rstd", [P, TILES], F32)
        neghalf = sb("neghalf", [P, TILES], F32)
        xn = sb("xn", [P, TILES, D], F32)
        xnT = sb("xnT", [D, N], F32)
        lgT = sb("lgT", [P, 512], F32)
        lg = sb("lg", [P, TILES, E], F32)
        top = sb("top", [P, TILES], F32)
        is_top = sb("is_top", [P, TILES, E], F32)
        first_top = sb("first_top", [P, TILES], F32)
        onehot = sb("onehot", [P, TILES, E], F32)
        onehotb = sb("onehotb", [P, TILES, E], BF16)
        tanh_half = sb("tanh_half", [P, TILES], F32)
        score = sb("score", [P, TILES], F32)
        table_use = sb("table_use", [P, 3], F32)
        over = sb("over", [P, E, 16], F32)
        etiles = sb("etiles", [P, E], F32)
        etb = sb("etb", [P, E, E], F32)
        estart128 = sb("estart128", [P, E], F32)
        eend = sb("eend", [P, E], F32)
        slot8 = sb("slot8", [P, TILES, E], F32)
        slotf = sb("slotf", [P, TILES], F32)
        slot = sb("slot", [P, TILES], U32)
        ended = sb("ended", [1, SLOT_TILES, E], F32)
        expertf = sb("expertf", [1, SLOT_TILES], F32)
        expert = sb("expert", [1, SLOT_TILES], I32)
        xs = sb("xs", [P, TILES, ROW], F32)
        sgate = sb("sgate", [P, 2, 512], F32)
        sh = sb("sh", [P, 2, 2, 512], F32)
        xg = sb("xg", [P, SLOT_TILES, ROW], F32)
        spare = sb("spare", [P, SLOT_TILES], I32)
        xgs = sb("xgs", [P, 2, D], F32)
        xgT = sb("xgT", [P, 2, P], F32)
        rsg = sb("rsg", [P, 2, F], F32)
        rh = sb("rh", [P, 2, F], F32)
        rhT = sb("rhT", [P, 2, 2, P], F32)
        ys = sb("ys", [P, SLOT_TILES, D], F32)
        yg = xs[:, :, 0:D]
        xs_dram = nc.dram_tensor("xs_sorted", (SLOT_TILES * P, ROW), F32, kind="Internal").ap()
        xs_slots = xs_dram.rearrange("(j p) d -> p j d", p=P)
        y_dram = nc.dram_tensor("y_by_token", (N + SLOT_TILES * P, D), F32, kind="Internal").ap()

        stats2 = sb("stats2", [P, 2, 6], F32)
        meanvar2 = sb("meanvar2", [P, 2, 2, 2], F32)
        rstd2 = sb("rstd2", [P, 2, 2], F32)
        xn2 = sb("xn2", [P, 2, 2, D], F32)
        xnT2 = sb("xnT2", [D, 2, L], F32)
        rc = sb("rc", [P, 2, 2 * D], F32)
        rs = sb("rs", [P, 2, 2 * D], F32)
        rot = sb("rot", [P, 2, 2 * D], F32)
        rem = sb("rem", [P, 2, 2 * D], F32)
        parts = [sb(f"parts{u}", [P, 2, 2, H, KROWS], BF16) for u in range(2)]
        qT = [sb(f"qT{u}", [P, H // 2, L], BF16) for u in range(2)]
        kT = [sb(f"kT{u}", [P, H // 2, 2, L], BF16) for u in range(2)]
        vstage = sb("vstage", [P, 2, 2, D], F32)
        vx = [sb(f"vx{u}", [P, 2, H, 32], F32) for u in range(2)]
        negmax = sb("negmax", [P, 2, 2, H], F32)
        mrem = sb("mrem", [P, 2, H // 2], F32)
        probs = sb("probs", [P, 8, 2 * L], F32)
        pvs = sb("pvs", [P, 2, L], F32)
        rden = sb("rden", [P, 16, 2], F32)
        oatt = sb("oatt", [P, 2, D], F32)
        oT = sb("oT", [D, L], F32)

        bank = [ctx.enter_context(nc.psum_tensor(f"bank{i}", [P, 512], F32)) for i in range(8)]
        work, sbank, stbank, pvbank = bank[0:2], bank[2:4], bank[4:7], bank[7]

        x_loaded = sems("x_loaded", CHUNKS)
        gate_loaded = sem("gate_loaded")
        tab_loaded, shw_loaded, rw_loaded, aw_loaded = (sem(n) for n in ("tab_loaded", "shw_loaded", "rw_loaded", "aw_loaded"))
        consts_set, slots_set, slots_cleared = sem("consts_set"), sem("slots_set"), sem("slots_cleared")
        ln_stats, ln_rstd, xn_ready = sem("ln_stats"), sem("ln_rstd"), sem("xn_ready")
        xT_filled, xT_copied = sem("xT_filled"), sem("xT_copied")
        lgT_filled, lgT_copied, lg_filled = (sem(n) for n in ("lgT_filled", "lgT_copied", "lg_filled"))
        top_ready, tanh_ready, score_ready, onehot_ready = (sem(n) for n in ("top_ready", "tanh_ready", "score_ready", "onehot_ready"))
        rank_filled, slot_ready, xs_ready, scattered = (sem(n) for n in ("rank_filled", "slot_ready", "xs_ready", "scattered"))
        expert_ready = sem("expert_ready")
        sg_filled, su_filled, ssilu, sh_ready, sy_filled, sy_added = (sem(n) for n in ("sg_filled", "su_filled", "ssilu", "sh_ready", "sy_filled", "sy_added"))
        xg_loaded = sems("xg_loaded", LOADS)
        xgs_ready = sem("xgs_ready")
        gT_filled, gT_copied, gu_filled, rsilu, rh_ready = (sem(n) for n in ("gT_filled", "gT_copied", "gu_filled", "rsilu", "rh_ready"))
        hT_filled, hT_copied, ry_filled, ys_ready = (sem(n) for n in ("hT_filled", "hT_copied", "ry_filled", "ys_ready"))
        y_scattered, y_loaded = sem("y_scattered"), sems("y_loaded", CHUNKS)
        ffn_added, out_stored = sem("ffn_added"), sem("out_stored")
        waited = sem("waited")
        dve_step, pool_step = sem("dve_step"), sem("pool_step")
        uses = ["back", "qa", "ka", "mb", "oT", "wo", "xT", "qb", "kb", "ma"]
        lag = dict(back=-1, qa=1, ka=1, mb=0, oT=-1, wo=-1, xT=3, qb=1, kb=1, ma=1)
        filled = {n: sem("filled_" + n) for n in uses + ["qkv0", "qkv1"]}
        emptied = {n: sem("emptied_" + n) for n in uses + ["qkv0", "qkv1"]}
        a_stats, a_rstd, a_xn = sem("a_stats"), sem("a_rstd"), sem("a_xn")
        roped, rotated, part1, rem_ready, part2, part3, vx_ready = (sem(n) for n in ("roped", "rotated", "part1", "rem_ready", "part2", "part3", "vx_ready"))
        s_filled, s_reduced, m_split = sem("s_filled"), sem("s_reduced"), sem("m_split")
        st_filled, exp_done, pv_done, pv_copied = sem("st_filled"), sem("exp_done"), sem("pv_done"), sem("pv_copied")

        def wait_apart(eng, s, value):
            eng.wait_ge(s, value)
            if not isinstance(value, int):
                eng.sem_inc(waited, 1)

        class Steps:

            def __init__(self, eng, s):
                self.eng, self.s, self.n, self.moved = eng, s, 0, 0

            def link(self, ins):
                ins.then_inc(self.s, 1)
                self.n += 1
                wait_apart(self.eng, self.s, self.n + self.moved)

            def loop(self, i, start, step, body, per, turns):
                first = self.n
                self.moved = (i - start) * (per // step)
                body()
                assert self.n == first + per, self.n - first
                self.n, self.moved = first + per * turns, 0

        PAR = 2
        FIRST_LOOPED, END_LOOPED = 2, B - 3 - (B - 3 - 2) % PAR

        class Turn:

            def __init__(self, i, u, looped):
                self.i, self.u, self.v, self.looped = i, u, 1 - u, looped
                has = lambda k: looped or 0 <= i + k < B
                self.e, self.m, self.pr, self.nx, self.nx2, self.f = (has(k) for k in (0, 1, 2, 3, 4, -1))

            def early(self, late):
                c = None if self.looped else self.i - late - (B - CHUNKS + 1)
                return c if c is not None and 0 <= c < CHUNKS - 1 else None

            def from_(self, first):
                return self.looped or self.i >= first

        HH = H // 2

        EARLY_TURNED = ((0, 2), (0, 4), (1, 2))

        def st_bank(u, h):
            return (h + u) % 3

        def st_before(u, h):
            return next(d for d in range(1, H) if st_bank(u if d <= h else 1 - u, (h - d) % H) == st_bank(u, h))

        def attention(eng, turn, steps=None, per=0):
            for i in range(-3, FIRST_LOOPED):
                turn(Turn(i, i % PAR, False))
            with eng.Fori(FIRST_LOOPED // PAR, END_LOOPED // PAR) as w:
                i = w * PAR

                def body():
                    for k in range(PAR):
                        turn(Turn(i + k, k, True))
                if steps is None:
                    body()
                else:
                    steps.loop(i, FIRST_LOOPED, PAR, body, per, (END_LOOPED - FIRST_LOOPED) // PAR)
            for i in range(END_LOOPED, B + 1):
                turn(Turn(i, i % PAR, False))

        GROUP = 4
        RLOOP = (3, SLOT_TILES - 4 - (SLOT_TILES - 7) % GROUP, GROUP)

        def routed(eng, turn, load=None):
            def group(j0, turns, has):
                experts = load(j0, turns) if load else None
                for k in range(turns):
                    turn(j0 + k, (RLOOP[0] + k) % 2, has(k), *([experts, k] if load else []))

            there = lambda j0: lambda k: lambda d: 0 <= j0 + k + d < SLOT_TILES
            group(-1, RLOOP[0] + 1, there(-1))
            with eng.Fori(*RLOOP) as j:
                group(j, GROUP, lambda k: lambda d: True)
            group(RLOOP[1], SLOT_TILES + 1 - RLOOP[1], there(RLOOP[1]))

        block = ctx.enter_context(nc.Block())

        @block.sync
        def _(sp):
            xv = x_in.rearrange("(c i p) d -> c p i d", p=P, i=CHUNK)
            sp.dma_start(x[:, 0:CHUNK, :], xv[0]).then_inc(x_loaded[0], 16)
            sp.dma_start(tab[:], tab_in).then_inc(tab_loaded, 16)
            sp.dma_start(tabb[:], tabb_in).then_inc(tab_loaded, 16)
            sp.dma_start(wgate[:], wgate_in).then_inc(gate_loaded, 16)
            for c in range(1, CHUNKS):
                sp.dma_start(x[:, c * CHUNK:(c + 1) * CHUNK, :], xv[c]).then_inc(x_loaded[c], 16)
            sp.dma_start(shgu[:], shgu_in).then_inc(shw_loaded, 16)
            sp.dma_start(shdn[:], shdn_in).then_inc(shw_loaded, 16)
            sp.wait_ge(slots_set, 1)
            sp.dma_start(xs_slots, xg[:]).then_inc(slots_cleared, 16)
            sp.dma_start(rgu[:], rgu_in).then_inc(rw_loaded, 16)
            sp.dma_start(rdn[:], rdn_in).then_inc(rw_loaded, 16)
            sp.dma_start(wqkv[:], wqkv_in).then_inc(aw_loaded, 16)
            sp.dma_start(wo[:], wo_in).then_inc(aw_loaded, 16)
            for n in range(2):
                sp.wait_ge(scattered, 16 * TILES * (n + 1))
                for k in range(LOADS):
                    j0, j1 = k * LOAD, min((k + 1) * LOAD, SLOT_TILES)
                    sp.dma_start(xg[:, j0:j1, :], xs_slots[:, j0:j1, :]).then_inc(xg_loaded[k], 16)
                if n == 0:
                    for k in range(LOADS):
                        sp.wait_ge(xg_loaded[k], 16)
                    sp.dma_start(xs_slots[:, :, D:ROW].bitcast(I32), spare[:].unsqueeze(2), allow_slow_non_contiguous=True).then_inc(slots_cleared, 16)
                sp.wait_ge(y_scattered, 16 * SLOT_TILES * (n + 1))
                yv = y_dram[0:N, :].rearrange("(c i p) d -> c p i d", p=P, i=CHUNK)
                for c in range(CHUNKS):
                    sp.dma_start(yg[:, c * CHUNK:(c + 1) * CHUNK, :], yv[c]).then_inc(y_loaded[c], 16)
            ov = out.rearrange("(c i p) d -> c p i d", p=P, i=CHUNK)
            for c in range(CHUNKS):
                sp.wait_ge(ffn_added, TILES + (c + 1) * CHUNK)
                sp.dma_start(ov[c], x[:, c * CHUNK:(c + 1) * CHUNK, :]).then_inc(out_stored, 16)
            sp.wait_ge(out_stored, 16 * CHUNKS)

        @block.gpsimd
        def _(pool):
            g = nc.gpsimd
            st = Steps(pool, pool_step)
            g.memset(neghalf[:], -0.5).then_inc(consts_set, 1)
            pool.wait_ge(consts_set, 1)

            def ffn_rstd(n, c):
                pool.wait_ge(ln_stats, n * CHUNKS + c + 1)
                s = slice(c * CHUNK, (c + 1) * CHUNK)
                st.link(g.tensor_scalar_add(rstd[:, s], meanvar[:, s, 1], EPS))
                g.tensor_tensor(rstd[:, s], rstd[:, s], neghalf[:, s], ALU.pow).then_inc(ln_rstd, 1)

            def scatter(n):
                pool.wait_ge(slot_ready, n + 1)
                pool.wait_ge(slots_cleared, 16 * (n + 1))
                for i in range(TILES):
                    pool.wait_ge(xs_ready, n * TILES + i + 1)
                    g.indirect_dma_start(
                        xs_dram, bass.IndirectOffsetOnAxis(ap=slot[:, i:i + 1], axis=0), xs[:, i, :], None,
                        bounds_check=SLOT_TILES * P - 1, oob_is_err=False).then_inc(scattered, 16)

            def experts_io(n):
                r = n * SLOT_TILES
                for j in range(-5, SLOT_TILES):
                    k = j + 5
                    if k < SLOT_TILES:
                        if k % LOAD == 0:
                            pool.wait_ge(xg_loaded[k // LOAD], 16 * (n + 1))
                        if k >= 2 or n:
                            pool.wait_ge(gT_filled, r + k - 1)
                        g.tensor_copy(xgs[:, k % 2, :], xg[:, k, 0:D]).then_inc(xgs_ready, 1)
                    if j >= 0:
                        pool.wait_ge(ys_ready, r + j + 1)
                        g.indirect_dma_start(
                            y_dram, bass.IndirectOffsetOnAxis(ap=xg[:, j, D:ROW].bitcast(U32), axis=0), ys[:, j, :], None,
                            bounds_check=N + SLOT_TILES * P - 1, oob_is_err=False).then_inc(y_scattered, 16)

            for c in range(CHUNKS):
                ffn_rstd(0, c)
            for u in range(2):
                g.memset(kT[u][:].bitcast(F32), 0.0).then_inc(consts_set, 1)
                g.memset(vx[u][:], 0.0).then_inc(consts_set, 1)
                g.memset(parts[u][:].bitcast(F32), 0.0).then_inc(consts_set, 1)
            pool.wait_ge(consts_set, 7)
            for u in range(2):
                v5 = vx[u][:].rearrange("p t (f s g) c -> p (t f) s g c", f=2, s=2)
                for s_ in range(2):
                    g.memset(v5[:, :, s_, :, 16 + s_:17 + s_], 1.0).then_inc(consts_set, 1)
                g.memset(parts[u][:, :, 1, :, MCOL:MCOL + 3], 1.0).then_inc(consts_set, 1)
            scatter(0)
            experts_io(0)

            def turn(T):
                i, u, v = T.i, T.u, T.v

                def split_max(half):
                    w, h0, unit = (u, HH, 2 * i + 1) if half == 0 else (v, 0, 2 * i + 2)
                    wait_apart(pool, s_reduced, 8 * unit + 8)
                    m = negmax[:, w, :, h0:h0 + HH]
                    mc = [parts[w][:, :, 0, h0:h0 + HH, MCOL + k] for k in range(3)]
                    st.link(g.tensor_copy(mc[0], m))
                    st.link(g.tensor_tensor(mrem[:], m, mc[0], ALU.subtract))
                    st.link(g.tensor_copy(mc[1], mrem[:]))
                    g.tensor_tensor(mc[2], mrem[:], mc[1], ALU.subtract).then_inc(m_split, 1)

                def rotate(t):
                    if t == 0:
                        if T.from_(0):
                            wait_apart(pool, filled["mb"], i + 1)
                        g.memset(parts[u][:, :, 0, :, MCOL:MCOL + 3], 0.0)
                    wait_apart(pool, roped, 2 * (i + 2) + t + 1)
                    g.tensor_tensor(rot[:, t, :], rc[:, t, :], rs[:, t, :], ALU.add).then_inc(rotated, 1)

                def remainder(t):
                    wait_apart(pool, part1, 2 * (i + 2) + t + 1)
                    r3 = lambda a: a[:, t, :].rearrange("p (q h d) -> p (q h) d", q=2, h=H)
                    flat = parts[u][:, t].rearrange("p q h c -> p (q h) c")
                    g.tensor_tensor(r3(rem), r3(rot), flat[:, :, 2 * DH:3 * DH], ALU.subtract).then_inc(rem_ready, 1)

                def third(t):
                    wait_apart(pool, part2, 2 * (i + 2) + t + 1)
                    for q, at in ((0, 3), (1, 0)):
                        ins = g.tensor_tensor(
                            parts[u][:, t, q, :, at * DH:(at + 1) * DH], rem[:, t, q * D:(q + 1) * D].rearrange("p (h d) -> p h d", h=H),
                            parts[u][:, t, q, :, 5 * DH:6 * DH], ALU.subtract)
                    ins.then_inc(part3, 1)

                def values(t):
                    vs = vstage[:, v, t, :].rearrange("p (f s g d) -> p f s g d", f=2, s=2, g=4)
                    vd = vx[v][:, t].rearrange("p (f s g) c -> p f s g c", f=2, s=2)
                    for k in range(2):
                        ins = g.tensor_copy(vd[:, :, k, :, k * DH:(k + 1) * DH], vs[:, :, k])
                    if t == 1:
                        ins.then_inc(vx_ready, 1)

                if T.m:
                    wait_apart(pool, emptied["qkv1"], i + 2)
                    if T.from_(1):
                        wait_apart(pool, pv_done, 4 * i)
                    values(0)
                    values(1)
                if T.nx:
                    wait_apart(pool, a_stats, i + 4)
                    st.link(g.tensor_scalar_add(rstd2[:, v, :], meanvar2[:, v, :, 1], EPS))
                    g.tensor_tensor(rstd2[:, v, :], rstd2[:, v, :], neghalf[:, 0:2], ALU.pow).then_inc(a_rstd, 1)
                if T.e:
                    split_max(0)
                if T.pr:
                    rotate(0)
                    rotate(1)
                if T.pr:
                    remainder(0)
                    remainder(1)
                    third(0)
                if T.m:
                    split_max(1)
                if T.pr:
                    third(1)
                if T.early(0) is not None:
                    ffn_rstd(1, T.early(0))

            attention(pool, turn, st, 2 * (1 + 6))
            ffn_rstd(1, CHUNKS - 1)
            scatter(1)
            experts_io(1)

        @block.scalar
        def _(act):
            a = nc.scalar

            def copy_chunk(n, c):
                act.wait_ge(xT_filled, n * CHUNKS + c + 1)
                a.copy(xnT[:, c * 512:(c + 1) * 512], bank[2 + c % 2][:]).then_inc(xT_copied, 1)

            def ffn(n):
                for c in range(CHUNKS - 1 if n else 0, CHUNKS):
                    copy_chunk(n, c)

                def silu(c):
                    act.wait_ge(sg_filled, n * CHUNKS + c + 1)
                    if n * CHUNKS + c:
                        act.wait_ge(sh_ready, n * CHUNKS + c)
                    for k in range(2):
                        ins = a.activation(sgate[:, k, :], bank[2 + k][:], ACT.Silu)
                        ins.then_inc(ssilu, 1)

                act.wait_ge(top_ready, n + 1)
                a.activation(tanh_half[:], top[:], ACT.Tanh, scale=0.5).then_inc(tanh_ready, 1)
                act.wait_ge(score_ready, n + 1)
                for i in range(TILES):
                    a.activation(xs[:, i, 0:D], xn[:, i, :], ACT.Copy, scale=score[:, i:i + 1]).then_inc(xs_ready, 1)
                    if i == 3:
                        silu(0)
                for c in range(1, CHUNKS):
                    silu(c)

                r = n * SLOT_TILES

                def copy_gT(j, u):
                    act.wait_ge(gT_filled, j + (r + 1))
                    a.copy(xgT[:, u, :], bank[u][:, 0:P]).then_inc(gT_copied, 1)

                def turn(j, u, has):
                    if has(1):
                        act.wait_ge(gu_filled, j + (r + 2))
                        if not isinstance(j, int) or j >= 1:
                            act.wait_ge(rh_ready, j + r)
                        a.activation(rsg[:, 1 - u, :], bank[3 - u][:, 0:F], ACT.Silu).then_inc(rsilu, 1)
                    if has(3):
                        copy_gT(j + 3, 1 - u)
                    if has(0):
                        act.wait_ge(hT_filled, j + (r + 1))
                        if not isinstance(j, int) or j >= 2 or n:
                            act.wait_ge(ry_filled, j + (r - 1))
                        a.copy(rhT[:, u, :, :].rearrange("p k s -> p (k s)"), bank[4 + u][:, 0:2 * P]).then_inc(hT_copied, 1)

                copy_gT(0, 0)
                copy_gT(1, 1)
                routed(act, turn)

            def turn(T):
                i, u, v = T.i, T.u, T.v

                def exponentials(h):
                    act.wait_ge(st_filled, 16 * i + h + 1)
                    if T.from_(1) or h >= 8:
                        act.wait_ge(pv_done, 4 * i + (h // 4 - 1))
                    a.activation(probs[:, h % 8, :], stbank[st_bank(u, h)][:], ACT.Exp, scale=float(DH) ** -0.5).then_inc(exp_done, 1)

                def copy_keys(half):
                    name = ("ka", "kb")[half]
                    act.wait_ge(filled[name], i + 2)
                    src = work[uses.index(name) % 2][:].bitcast(BF16).rearrange("p (r s) -> p r s", r=4)
                    for k in range(2):
                        ins = a.copy(kT[v][64 * k:64 * k + 64, 4 * half:4 * half + 4, k, :], src[64 * k:64 * k + 64])
                    ins.then_inc(emptied[name], 1)

                def part(t, rows, src, into, ready, done):
                    act.wait_ge(ready, 2 * (i + 2) + t + 1)
                    if ready is rotated and T.from_(0):
                        act.wait_ge(filled["mb"], i + 1)
                    for q in range(2):
                        part_of = src[:, t, q * D:(q + 1) * D].rearrange("p (h d) -> p h d", h=H)
                        dst = parts[u][:, t, q, :, 0:MCOL].rearrange("p h (s d) -> p h s d", s=6)[:, :, into[q], :]
                        ins = a.copy(dst, part_of.unsqueeze(2).to_broadcast([P, H, rows, DH]))
                    ins.then_inc(done, 1)

                first = lambda t: part(t, 3, rot, (slice(0, 6, 2), slice(1, 4)), rotated, part1)
                second = lambda t: part(t, 2, rem, (slice(1, 6, 4), slice(4, 6)), rem_ready, part2)
                for half in range(2):
                    for s_ in range(HH):
                        if T.e:
                            exponentials(HH * half + s_)
                        if (half, s_) == (0, 1) and T.f:
                            act.wait_ge(pv_done, 4 * i)
                            a.copy(pvs[:].rearrange("p f s -> p (f s)"), pvbank[:]).then_inc(pv_copied, 1)
                        if (half, s_) == (1, 2) and T.f:
                            act.wait_ge(filled["oT"], i)
                            a.copy(oT[:], work[0][:, 0:L]).then_inc(emptied["oT"], 1)
                        if (half, s_) == (1, 7) and T.nx:
                            act.wait_ge(filled["xT"], i + 4)
                            a.copy(xnT2[:, v, :], work[0][:, 0:L]).then_inc(emptied["xT"], 1)
                        if not T.looped and i == B and (half, s_) in EARLY_TURNED:
                            copy_chunk(1, EARLY_TURNED.index((half, s_)))
                            if half:
                                a.activation(table_use[:, 2:3], neghalf[:, 0:1], ACT.Tanh)
                        if half and T.pr:
                            if s_ < 2:
                                first(s_)
                            if s_ in (3, 4):
                                second(s_ - 3)
                    if T.m:
                        copy_keys(half)

            act.wait_ge(consts_set, 1)
            a.activation(table_use[:, 0:1], neghalf[:, 0:1], ACT.Tanh)
            ffn(0)
            a.activation(table_use[:, 1:2], neghalf[:, 0:1], ACT.Exp)
            attention(act, turn)
            ffn(1)

        @block.vector
        def _(dve):
            v_ = nc.vector
            st = Steps(dve, dve_step)

            def normalise(o_, x_, mv, r_):
                return v_.tensor_scalar(o_, x_, mv, r_, ALU.subtract, ALU.mult)

            def moments(n, c):
                if n == 0:
                    dve.wait_ge(x_loaded[c], 16)
                else:
                    dve.wait_ge(emptied["wo"], 2 * c + 2)
                for i in range(c * CHUNK, (c + 1) * CHUNK):
                    ins = v_.bn_stats(stats[:, i, :], x[:, i, :])
                st.link(ins)
                for i in range(c * CHUNK, (c + 1) * CHUNK):
                    ins = v_.bn_aggr(meanvar[:, i, :], stats[:, i, :])
                ins.then_inc(ln_stats, 1)

            def normalise_chunk(n, c):
                dve.wait_ge(ln_rstd, n * CHUNKS + c + 1)
                for i in range(c * CHUNK, (c + 1) * CHUNK):
                    ins = normalise(xn[:, i, :], x[:, i, :], meanvar[:, i, 0:1], rstd[:, i:i + 1])
                    ins.then_inc(xn_ready, 1)

            def ffn(n):
                for c in range(CHUNKS - 1 if n else 0, CHUNKS):
                    if n or c:
                        moments(n, c)
                    if c and not n:
                        normalise_chunk(n, c - 1)
                normalise_chunk(n, CHUNKS - 1)

                dve.wait_ge(lgT_filled, n + 1)
                v_.tensor_copy(lgT[:], bank[7][:]).then_inc(lgT_copied, 1)
                dve.wait_ge(lg_filled, n + 1)
                src = bank[0][:].rearrange("p (c g k) -> p g c k", c=4, g=4)[:, :, :, 0:E]
                st.link(v_.tensor_copy(lg[:].rearrange("p (g c) e -> p g c e", g=4), src))
                lg_all = lambda a_: a_[:].unsqueeze(2).to_broadcast([P, TILES, E])
                v_.tensor_reduce(top[:], lg[:], AX.X, ALU.max).then_inc(top_ready, 1)
                dve.wait_ge(top_ready, n + 1)
                st.link(v_.tensor_tensor(is_top[:], lg[:], lg_all(top), ALU.is_equal))
                em8 = eminus8.unsqueeze(1).to_broadcast([P, TILES, E])
                st.link(v_.tensor_tensor(is_top[:], is_top[:], em8, ALU.mult))
                st.link(v_.tensor_reduce(first_top[:], is_top[:], AX.X, ALU.min))
                st.link(v_.tensor_tensor(onehot[:], em8, lg_all(first_top), ALU.is_equal))
                v_.tensor_copy(onehotb[:], onehot[:]).then_inc(onehot_ready, 1)
                dve.wait_ge(tanh_ready, n + 1)
                v_.tensor_scalar(score[:], tanh_half[:], 0.5, 0.5, ALU.mult, ALU.add).then_inc(score_ready, 1)

                def shared_hidden(c):
                    k0 = n * CHUNKS + c
                    dve.wait_ge(ssilu, 2 * k0 + 2)
                    if k0 >= 2:
                        dve.wait_ge(sy_filled, k0 - 1)
                    for k in range(2):
                        dve.wait_ge(su_filled, 2 * k0 + k + 1)
                        ins = v_.tensor_tensor(sh[:, c % 2, k, :], sgate[:, k, :], bank[4 + k][:], ALU.mult)
                    ins.then_inc(sh_ready, 1)

                def shared_add(c):
                    dve.wait_ge(sy_filled, n * CHUNKS + c + 1)
                    s = slice(c * CHUNK, (c + 1) * CHUNK)
                    xc = x[:, s, :].rearrange("p i d -> p (i d)")
                    v_.scalar_tensor_tensor(out=xc, in0=bank[6][:], scalar=0.5, in1=xc, op0=ALU.mult, op1=ALU.add).then_inc(sy_added, 1)

                dve.wait_ge(rank_filled, n + 1)
                rank = bank[7][:, 0:(TILES + 1) * E].rearrange("p (i e) -> p i e", e=E)
                st.link(v_.tensor_tensor(over[:], rank[:, TILES, :].unsqueeze(2).to_broadcast([P, E, 16]),
                                         steps128.unsqueeze(1).to_broadcast([P, E, 16]), ALU.is_gt))
                st.link(v_.tensor_reduce(etiles[:], over[:], AX.X, ALU.add))
                st.link(v_.tensor_tensor(etb[:], before, etiles[:].unsqueeze(1).to_broadcast([P, E, E]), ALU.mult))
                st.link(v_.tensor_reduce(estart128[:], etb[:], AX.X, ALU.add))
                st.link(v_.tensor_tensor(slot8[:], rank[:, 0:TILES, :], estart128[:].unsqueeze(1).to_broadcast([P, TILES, E]), ALU.add))
                st.link(v_.tensor_tensor(slot8[:], slot8[:], onehot[:], ALU.mult))
                st.link(v_.tensor_reduce(slotf[:], slot8[:], AX.X, ALU.add))
                v_.tensor_copy(slot[:], slotf[:]).then_inc(slot_ready, 1)
                st.link(v_.scalar_tensor_tensor(out=eend[:], in0=estart128[:], scalar=1.0 / P, in1=etiles[:], op0=ALU.mult, op1=ALU.add))
                st.link(v_.tensor_tensor(ended[:], eend[0:1, :].unsqueeze(1).to_broadcast([1, SLOT_TILES, E]),
                                         tile_no[0:1, :].unsqueeze(2).to_broadcast([1, SLOT_TILES, E]), ALU.is_le))
                st.link(v_.tensor_reduce(expertf[:], ended[:], AX.X, ALU.add))
                st.link(v_.tensor_scalar(expertf[:], expertf[:], float(E - 1), None, ALU.min))
                v_.tensor_copy(expert[:], expertf[:]).then_inc(expert_ready, 1)

                shared_hidden(0)
                for c in range(1, CHUNKS):
                    shared_add(c - 1)
                    shared_hidden(c)
                shared_add(CHUNKS - 1)

                r = n * SLOT_TILES

                def turn(j, u, has):
                    if has(1):
                        dve.wait_ge(rsilu, j + (r + 2))
                        if not isinstance(j, int) or j >= 1 or n:
                            dve.wait_ge(hT_filled, j + r)
                        v_.tensor_tensor(rh[:, 1 - u, :], rsg[:, 1 - u, :], bank[3 - u][:, F:2 * F], ALU.mult).then_inc(rh_ready, 1)
                    if has(-1):
                        dve.wait_ge(ry_filled, j + r)
                        v_.tensor_copy(ys[:, bass.ds(j - 1, 1), :].rearrange("p a d -> p (a d)"), bank[6 + (1 - u)][:, 0:D]).then_inc(ys_ready, 1)

                routed(dve, turn)
                if n:
                    add_experts(n, 0, TILES)

            def add_experts(n, i0, i1):
                if i0 == 0:
                    dve.wait_ge(sy_added, CHUNKS * (n + 1))
                while i0 < i1:
                    i = min(i1, (i0 // CHUNK + 1) * CHUNK)
                    dve.wait_ge(y_loaded[i0 // CHUNK], 16 * (n + 1))
                    v_.scalar_tensor_tensor(out=x[:, i0:i, :], in0=yg[:, i0:i, :], scalar=0.5, in1=x[:, i0:i, :],
                                            op0=ALU.mult, op1=ALU.add).then_inc(ffn_added, i - i0)
                    i0 = i

            def turn(T):
                i, u, v = T.i, T.u, T.v

                def copy_queries(name):
                    w, seq = (u, i) if name == "mb" else (v, i + 1)
                    h0 = 0 if name[1] == "a" else 4
                    dve.wait_ge(filled[name], seq + 1)
                    v_.tensor_copy(qT[w][:, h0:h0 + 4, :].rearrange("p r s -> p (r s)"),
                                   work[uses.index(name) % 2][:].bitcast(BF16)).then_inc(emptied[name], 1)

                def maxima(half, k):
                    w, h0, unit = (u, HH, 2 * i + 1) if half == 0 else (v, 0, 2 * i + 2)
                    dve.wait_ge(s_filled, 8 * unit + k + 1)
                    pair, t = k // 2, k % 2
                    v_.tensor_reduce(negmax[:, w, t, h0 + 2 * pair:h0 + 2 * pair + 2], sbank[k % 2][:].rearrange("p (a s) -> p a s", a=2),
                                     AX.X, ALU.max, negate=True).then_inc(s_reduced, 1)

                def rope(t):
                    name = f"qkv{t}"
                    dve.wait_ge(filled[name], i + 3)
                    if T.from_(-1):
                        dve.wait_ge(rotated, 2 * (i + 1) + t + 1)
                    qk = sbank[t][:, 0:2 * D]
                    heads = lambda a_: a_.rearrange("p (h d) -> p h d", d=DH)
                    pairs = lambda a_: a_.rearrange("p (h r two) -> p h r two", r=DH // 2, two=2)
                    sn = sin[:, t, :].rearrange("p (r two) -> p r two", two=2)
                    v_.tensor_tensor(heads(rc[:, t, :]), heads(qk), cos[:, t, :].unsqueeze(1).to_broadcast([P, 2 * H, DH]), ALU.mult)
                    for odd in range(2):
                        ins = v_.tensor_tensor(pairs(rs[:, t, :])[:, :, :, odd], pairs(qk)[:, :, :, 1 - odd],
                                               sn[:, :, odd].unsqueeze(1).to_broadcast([P, 2 * H, DH // 2]), ALU.mult)
                    ins.then_inc(roped, 1)
                    if T.from_(0):
                        dve.wait_ge(vx_ready, i + 1)
                    v_.tensor_copy(vstage[:, u, t, :], sbank[t][:, 2 * D:3 * D]).then_inc(emptied[name], 1)

                def tile(t, w=1):
                    return x[:, bass.ds(t, w), :].rearrange("p a d -> p (a d)")

                if not T.looped and i < 0:
                    add_experts(0, *((0, 4), (4, 10), (10, 16))[i + 3])
                def moments_of(k, w):
                    dve.wait_ge(ffn_added, 2 * (i + k) + 2)
                    for t in range(2):
                        ins = v_.bn_stats(stats2[:, t, :], tile(2 * (i + k) + t))
                    st.link(ins)
                    for t in range(2):
                        ins = v_.bn_aggr(meanvar2[:, w, t, :], stats2[:, t, :])
                    ins.then_inc(a_stats, 1)

                if not T.looped and i == -3:
                    moments_of(3, v)

                def divide():
                    dve.wait_ge(filled["back"], i)
                    bk = work[uses.index("back") % 2][:]
                    st.link(v_.reciprocal(rden[:], bk.rearrange("p (x c) -> p x c", x=16)[:, :, 16:18]))
                    bk = bk.rearrange("p (x g c) -> p x g c", x=4, g=4)
                    ov = oatt[:].rearrange("p t (f s g d) -> p (t f) s g d", f=2, s=2, g=4)
                    rv = rden[:].rearrange("p (x g) s -> p x g s", x=4)
                    for k in range(2):
                        ins = v_.tensor_tensor(ov[:, :, k], bk[:, :, :, k * DH:(k + 1) * DH],
                                               rv[:, :, :, k].unsqueeze(3).to_broadcast([P, 4, 4, DH]), ALU.mult)
                    ins.then_inc(emptied["back"], 1)

                for half in range(2):
                    for s_ in range(HH):
                        if (T.m if half else T.e):
                            maxima(half, s_)
                        if (half, s_) == (0, 4) and T.f:
                            divide()
                        if (half, s_) == (1, 2) and T.nx:
                            dve.wait_ge(a_rstd, i + 4)
                            for t in range(2):
                                ins = normalise(xn2[:, v, t, :], tile(2 * (i + 3) + t), meanvar2[:, v, t, 0:1], rstd2[:, v, t:t + 1])
                                ins.then_inc(a_xn, 1)
                        if (half, s_) == (1, 6) and T.f:
                            dve.wait_ge(filled["wo"], i)
                            v_.tensor_tensor(tile(2 * (i - 1), 2), work[1][:, 0:L], tile(2 * (i - 1), 2), ALU.add).then_inc(emptied["wo"], 1)
                    if T.m:
                        copy_queries(("qa", "qb")[half])
                    if half == 0:
                        if T.e:
                            copy_queries("mb")
                        if T.pr:
                            rope(0)
                            rope(1)
                    else:
                        if T.nx2:
                            moments_of(4, u)
                        if T.m:
                            copy_queries("ma")
                    if half == 0 and T.early(1) is not None:
                        normalise_chunk(1, T.early(1))
                    if half and T.early(0) is not None:
                        moments(1, T.early(0))

            st.link(v_.memset(xg[:], 0.0))
            moments(0, 0)
            dve.wait_ge(tab_loaded, 32)
            v_.tensor_copy(xg[:, :, D].bitcast(I32), spare_no).then_inc(slots_set, 1)
            v_.tensor_copy(spare[:], spare_no)
            v_.tensor_copy(xs[:, :, D].bitcast(I32), token_no)
            ffn(0)
            attention(dve, turn, st, 2 * 2)
            ffn(1)

        @block.tensor
        def _(pe):
            t_ = nc.tensor

            def mm(o_, l, r, start=True, stop=True, **k):
                return t_.matmul(o_, l, r, start=start, stop=stop, **k)

            def turn_chunk(n, c):
                pe.wait_ge(xn_ready, (n * CHUNKS + c + 1) * CHUNK)
                if c >= 2:
                    pe.wait_ge(xT_copied, n * CHUNKS + c - 1)
                for i in range(CHUNK):
                    ins = t_.transpose(bank[2 + c % 2][:, i * P:(i + 1) * P], xn[:, c * CHUNK + i, :], ident)
                ins.then_inc(xT_filled, 1)

            def logits(n, c):
                if n == 0 and c == 0:
                    pe.wait_ge(gate_loaded, 16)
                pe.wait_ge(xT_copied, n * CHUNKS + c + 1)
                return mm(bank[7][32 * c:32 * c + 32, :], wgate[:], xnT[:, c * 512:(c + 1) * 512])

            def ffn(n):
                if n == 0:
                    pe.wait_ge(tab_loaded, 32)
                else:
                    pe.wait_ge(emptied["wo"], B)
                    pe.wait_ge(exp_done, 16 * B)
                for c in range(CHUNKS):
                    if c:
                        logits(n, c - 1)
                    if n == 0 or c == CHUNKS - 1:
                        turn_chunk(n, c)
                logits(n, CHUNKS - 1).then_inc(lgT_filled, 1)
                pe.wait_ge(lgT_copied, n + 1)
                for c in range(4):
                    ins = t_.transpose(bank[0][:, c * P:(c + 1) * P], lgT[:, c * P:(c + 1) * P], ident)
                ins.then_inc(lg_filled, 1)

                def shared_gate(c, halves=range(2)):
                    k0 = n * CHUNKS + c
                    if k0:
                        pe.wait_ge(ssilu, 2 * k0)
                    for k in halves:
                        ins = mm(bank[2 + k][:], shgu[:, k * P:(k + 1) * P], xnT[:, c * 512:(c + 1) * 512])
                    if k:
                        ins.then_inc(sg_filled, 1)

                def shared_up(c):
                    k0 = n * CHUNKS + c
                    if k0:
                        pe.wait_ge(sh_ready, k0)
                    for k in range(2):
                        mm(bank[4 + k][:], shgu[:, F + k * P:F + (k + 1) * P], xnT[:, c * 512:(c + 1) * 512]).then_inc(su_filled, 1)

                def shared_down(c):
                    k0 = n * CHUNKS + c
                    pe.wait_ge(sh_ready, k0 + 1)
                    if k0:
                        pe.wait_ge(sy_added, k0)
                    for i in range(CHUNK):
                        for k in range(2):
                            ins = mm(bank[6][:, i * P:(i + 1) * P], sh[:, c % 2, k, i * P:(i + 1) * P], shdn[:, k, :],
                                     start=(k == 0), stop=(k == 1))
                    ins.then_inc(sy_filled, 1)

                if n == 0:
                    pe.wait_ge(shw_loaded, 32)
                shared_gate(0, [0])
                pe.wait_ge(onehot_ready, n + 1)
                rank = bank[7][:, 0:(TILES + 1) * E]
                oh = onehotb[:]
                mm(rank[:, 0:TILES * E], upper, oh.rearrange("p i e -> p (i e)"), stop=False, skip_group_check=True)
                for i in range(TILES):
                    w = TILES - i
                    ins = mm(rank[:, (i + 1) * E:].rearrange("p (i e) -> p i e", e=E), onesb,
                             oh[:, i:i + 1, :].to_broadcast([P, w, E]), start=False, stop=(i == TILES - 1), skip_group_check=True)
                ins.then_inc(rank_filled, 1)
                shared_gate(0, [1])
                shared_up(0)
                for c in range(1, CHUNKS):
                    shared_gate(c)
                    shared_down(c - 1)
                    shared_up(c)
                shared_down(CHUNKS - 1)

                r = n * SLOT_TILES
                if n == 0:
                    pe.wait_ge(rw_loaded, 32)
                pe.wait_ge(expert_ready, n + 1)

                def turn_g(j, u):
                    pe.wait_ge(xgs_ready, j + (r + 1))
                    if not isinstance(j, int) or j >= 2:
                        pe.wait_ge(gT_copied, j + (r - 1))
                    t_.transpose(bank[u][:, 0:P], xgs[:, u, :], ident).then_inc(gT_filled, 1)

                def load_experts(j0, turns):
                    low = max(j0 - 1, 0) if isinstance(j0, int) else j0 - 1
                    count = turns + 2 if not isinstance(j0, int) else min(j0 + turns + 1, SLOT_TILES) - low
                    pe.load(expert_regs[0:count], expert[0:1, bass.ds(low, count)])
                    values = [t_.snap(r_, min_val=0, max_val=E - 1) for r_ in expert_regs[0:count]]
                    return values, (low - j0 if isinstance(j0, int) else -1)

                def turn(j, u, has, experts, k_):
                    values, first_ = experts
                    if has(1):
                        ex = values[k_ + 1 - first_]
                        pe.wait_ge(gT_copied, j + (r + 2))
                        if not isinstance(j, int) or j >= 1 or n:
                            pe.wait_ge(rh_ready, j + r)
                        mm(bank[3 - u][:], xgT[:, 1 - u, :], rgu[:, bass.ds(ex * (2 * F), 2 * F)]).then_inc(gu_filled, 1)
                    if has(3):
                        turn_g(j + 3, 1 - u)
                    if has(0):
                        pe.wait_ge(rh_ready, j + (r + 1))
                        for k in range(2):
                            ins = t_.transpose(bank[4 + u][:, k * P:(k + 1) * P], rh[:, u, k * P:(k + 1) * P], ident)
                        ins.then_inc(hT_filled, 1)
                    if has(-1):
                        v = 1 - u
                        ex = values[k_ - 1 - first_]
                        pe.wait_ge(hT_copied, j + r)
                        if not isinstance(j, int) or j >= 3:
                            pe.wait_ge(ys_ready, j + (r - 2))
                        for k in range(2):
                            ins = mm(bank[6 + v][:, 0:D], rhT[:, v, k, :], rdn[:, bass.ds(ex * (2 * D) + k * D, D)], start=(k == 0), stop=(k == 1))
                        ins.then_inc(ry_filled, 1)

                turn_g(0, 0)
                turn_g(1, 1)
                routed(pe, turn, load_experts)

            def turn(T):
                i, u, v = T.i, T.u, T.v

                def work_bank(name):
                    at = uses.index(name)
                    for back in range(2, 3 * len(uses), 2):
                        before_ = uses[(at - back) % len(uses)]
                        seq = i - (back - at + len(uses) - 1) // len(uses) + lag[before_]
                        if T.looped or 0 <= seq < B:
                            pe.wait_ge(emptied[before_], seq + 1)
                            break
                    return work[at % 2]

                def turn_parts(name):
                    w = u if name == "mb" else v
                    q, h0 = int(name[0] == "k"), 0 if name[1] == "a" else HH
                    to = work_bank(name)[:].bitcast(BF16)
                    for pair in range(4):
                        for t in range(2):
                            h = h0 + 2 * pair
                            at = (2 * pair + t) * P
                            ins = t_.transpose(to[:, at:at + P], parts[w][:, t, q, h:h + 2, :].rearrange("p a c -> p (a c)"), identb)
                    ins.then_inc(filled[name], 1)

                def scores(half, k):
                    w, h0, unit = (u, 4, 2 * i + 1) if half == 0 else (v, 0, 2 * i + 2)
                    if k == 0:
                        for name in (("qb", "kb"), ("qa", "ka"))[half]:
                            pe.wait_ge(emptied[name], i + 1 + half)
                    if k < 2 and half and T.pr:
                        pe.wait_ge(emptied[f"qkv{k}"], i + 3)
                    elif k >= 2 or half == 0 or T.from_(0):
                        pe.wait_ge(s_reduced, 8 * unit + (k - 1))
                    pair, t = k // 2, k % 2
                    mm(sbank[k % 2][:], qT[w][:, h0 + pair, t * P:(t + 1) * P],
                       kT[w][:, h0 + pair, :, :].rearrange("p a s -> p (a s)")).then_inc(s_filled, 1)

                def scores_t(h):
                    if h % HH == 0:
                        pe.wait_ge(emptied[("ma", "mb")[h // HH]], i + 1)
                    back = st_before(u, h)
                    if T.from_(1) or h >= back:
                        pe.wait_ge(exp_done, 16 * i + (h - back + 1))
                    for k in range(2):
                        ins = mm(stbank[st_bank(u, h)][:, k * L:(k + 1) * L], kT[u][:, h // 2, h % 2, k * P:(k + 1) * P], qT[u][:, h // 2, :])
                    ins.then_inc(st_filled, 1)

                def values(k, c):
                    if c == 0:
                        if k == 0:
                            pe.wait_ge(vx_ready, i + 1)
                            if T.from_(1):
                                pe.wait_ge(pv_copied, i)
                        pe.wait_ge(exp_done, 16 * i + 4 * k + 4)
                    f_, s2 = k // 2, k % 2
                    for g in range(4):
                        h = 4 * k + g
                        ins = mm(pvbank[32 * g:32 * g + 32, f_ * L:(f_ + 1) * L], vx[u][:, c, h, :],
                                 probs[:, h % 8, c * L:(c + 1) * L], start=(s2 == 0 and c == 0), stop=(s2 == 1 and c == 1))
                    if c == 1:
                        ins.then_inc(pv_done, 1)

                def project(t):
                    if t == 0:
                        pe.wait_ge(emptied["xT"], i + 3)
                    if T.e:
                        pe.wait_ge(s_reduced, 16 * (i + 1))
                    mm(sbank[t][:, 0:3 * D], xnT2[:, u, t * P:(t + 1) * P], wqkv[:]).then_inc(filled[f"qkv{t}"], 1)

                for half in range(2):
                    for s_ in range(HH):
                        if not T.looped and i == B and (half, s_) in EARLY_TURNED:
                            pe.wait_ge(s_reduced, 16 * B)
                            turn_chunk(1, EARLY_TURNED.index((half, s_)))
                        if T.e:
                            scores_t(HH * half + s_)
                            if s_ in (6, 7):
                                values(2 * half, int(s_ == 7))
                        if (T.m if half else T.e):
                            scores(half, s_)
                        if (half, s_) == (0, 3) and T.f:
                            w = work_bank("back")
                            pe.wait_ge(pv_copied, i)
                            for c in range(4):
                                ins = t_.transpose(w[:, c * P:(c + 1) * P], pvs[:, c % 2, (c // 2) * P:(c // 2 + 1) * P], ident)
                            ins.then_inc(filled["back"], 1)
                        if (half, s_) == (1, 1) and T.f:
                            w = work_bank("oT")
                            pe.wait_ge(emptied["back"], i)
                            for t in range(2):
                                ins = t_.transpose(w[:, t * P:(t + 1) * P], oatt[:, t, :], ident)
                            ins.then_inc(filled["oT"], 1)
                        if (half, s_) == (1, 5) and T.f:
                            w = work_bank("wo")
                            pe.wait_ge(emptied["oT"], i)
                            for t in range(2):
                                ins = mm(w[:, t * P:(t + 1) * P], oT[:, t * P:(t + 1) * P], wo[:])
                            ins.then_inc(filled["wo"], 1)
                        if (half, s_) == (1, 6) and T.nx:
                            w = work_bank("xT")
                            pe.wait_ge(a_xn, 2 * (i + 3) + 2)
                            for t in range(2):
                                ins = t_.transpose(w[:, t * P:(t + 1) * P], xn2[:, v, t, :], ident)
                            ins.then_inc(filled["xT"], 1)
                    if T.m:
                        if half == 0:
                            pe.wait_ge(part3, 2 * (i + 1) + 2)
                        turn_parts(("qa", "qb")[half])
                        turn_parts(("ka", "kb")[half])
                    if T.e:
                        values(2 * half + 1, 0)
                        if half == 0:
                            values(2 * half + 1, 1)
                    if (T.m if half else T.e):
                        pe.wait_ge(m_split, 2 * i + half + 2)
                        turn_parts(("mb", "ma")[half])
                    if T.e and half:
                        values(2 * half + 1, 1)
                    if half == 0 and T.pr:
                        project(0)
                        project(1)

            expert_regs = [pe.alloc_register(f"expert{k}") for k in range(GROUP + 2)]
            ffn(0)
            pe.wait_ge(aw_loaded, 32)
            for s_ in (gT_copied, rh_ready, hT_copied, ys_ready):
                pe.wait_ge(s_, SLOT_TILES)
            attention(pe, turn)
            ffn(1)


TAB_COLS = P + 4 * DH + 88 + 2 * SLOT_TILES + TILES
TABB_COLS = 3 * P


def tables():
    f = np.float32
    freqs = np.exp((-np.log(10000.0)).astype(f) * np.arange(0, DH, 2, dtype=f) / f(DH)).astype(f)
    angle = (np.arange(L, dtype=f)[:, None] * freqs).astype(f)
    by_tile = lambda a: a.reshape(2, P, DH).transpose(1, 0, 2).reshape(P, 2 * DH)
    cos = by_tile(np.repeat(np.cos(angle), 2, axis=1))
    sin = by_tile(np.stack([-np.sin(angle), np.sin(angle)], axis=-1))
    row = lambda a: np.tile(np.asarray(a, f).reshape(1, -1), (P, 1))
    tab = np.concatenate([np.eye(P, dtype=f), cos, sin, row(np.arange(16) * P), row(np.tril(np.full((E, E), P), -1)),
                          row(np.arange(E) - E), row(np.arange(SLOT_TILES)),
                          np.arange(N + SLOT_TILES * P, dtype=f).reshape(-1, P).T], axis=1)
    tabb = np.concatenate([np.eye(P), np.triu(np.ones((P, P)), 1), np.ones((P, P))], axis=1)
    return np.ascontiguousarray(tab, f), tabb


def kernel(L0_attn_x, L0_attn_W_q, L0_attn_W_k, L0_attn_W_v, L0_attn_W_o, L0_ffn_gate_w, L0_ffn_shared_gate,
           L0_ffn_shared_up, L0_ffn_shared_down, L0_ffn_r_gate, L0_ffn_r_up, L0_ffn_r_down):
    import ml_dtypes
    import concourse.bacc as bacc
    from concourse.bass_utils import run_bass_kernel_spmd as run

    tab, tabb = tables()
    gate = np.zeros((D, 32), np.float32)
    gate[:, 0:E] = np.transpose(L0_ffn_gate_w)
    cols = lambda *a: np.concatenate([np.transpose(w) for w in a], axis=1)
    two = np.concatenate([np.transpose(L0_ffn_r_gate, (2, 0, 1)), np.transpose(L0_ffn_r_up, (2, 0, 1))], axis=2)
    arrays = {
        "x": np.reshape(L0_attn_x, (N, D)),
        "wqkv": cols(L0_attn_W_q, L0_attn_W_k, L0_attn_W_v),
        "wo": np.transpose(L0_attn_W_o),
        "wgate": gate,
        "shgu": cols(L0_ffn_shared_gate, L0_ffn_shared_up),
        "shdn": np.transpose(np.reshape(np.transpose(L0_ffn_shared_down), (2, P, D)), (1, 0, 2)),
        "rgu": np.reshape(two, (D, E * 2 * F)),
        "rdn": np.reshape(np.transpose(np.reshape(L0_ffn_r_down, (E, D, 2, P)), (3, 0, 2, 1)), (P, E * 2 * D)),
        "tab": tab,
        "tabb": tabb.astype(ml_dtypes.bfloat16),
    }
    arrays = {k: np.ascontiguousarray(v) for k, v in arrays.items()}
    nc = bacc.Bacc("TRN2", target_bir_lowering=False, num_devices=1)
    aps = [nc.dram_tensor("in_" + k, v.shape, mybir.dt.from_np(v.dtype), kind="ExternalInput").ap() for k, v in arrays.items()]
    out = nc.dram_tensor("out_x", (N, D), F32, kind="ExternalOutput").ap()
    build(nc, *aps, out)
    r = run(nc, [{"in_" + k: v for k, v in arrays.items()}], core_ids=[0])
    return np.reshape(r.results[0]["out_x"], (B, L, D))
```
